# Optimizing a Trainium2 kernel written in Bass

```python
import numpy as np
import jax
import jax.numpy as jnp

def _softmax(x, axis=-1):
    return jax.nn.softmax(x, axis=axis)

def _gelu(x):
    return jax.nn.gelu(x, approximate=True)

def _silu(x):
    return jax.nn.silu(x)

def _sigmoid(x):
    return jax.nn.sigmoid(x)

def _layernorm(x, axis=-1, eps=1e-05):
    m = jnp.mean(x, axis=axis, keepdims=True)
    v = jnp.var(x, axis=axis, keepdims=True)
    return (x - m) / jnp.sqrt(v + eps)

def _scatter_add(tgt, idx, src, axis=0):
    return tgt.at[idx].add(src)

def _segment_sum(src, seg, n):
    return jax.ops.segment_sum(src, seg, n)
kernel_name = 'mk_prb_d1_jaxref_r4_b799e8'

def setup_inputs(seed: int=0):
    np.random.seed(seed)
    _w = jnp.asarray

    def _L0_attn_setup():
        import jax, jax.numpy as jnp
        import numpy as np
        D_MODEL = 256
        NUM_HEADS = 16
        D_K = D_MODEL // NUM_HEADS
        THETA = 10000.0
        NEG_INF = -1000000000.0

        def _rope(x, positions):
            half = D_K // 2
            inv_freq = 1.0 / THETA ** (jnp.arange(0, D_K, 2, dtype=jnp.float32) / D_K)
            angles = positions.astype(jnp.float32)[:, None] * inv_freq
            cos, sin = (jnp.cos(angles), jnp.sin(angles))
            xe = x[..., 0::2]
            xo = x[..., 1::2]
            re = xe * cos - xo * sin
            ro = xe * sin + xo * cos
            return jnp.stack([re, ro], axis=-1).reshape(x.shape).astype(x.dtype)
        key = jax.random.key(seed)
        ks = jax.random.split(key, 5)
        sigma = np.sqrt(2.0 / (D_MODEL + D_MODEL))
        x = jax.random.normal(ks[0], (2, 512, D_MODEL), dtype=jnp.float32)
        mk = lambda k: (sigma * jax.random.normal(k, (D_MODEL, D_MODEL))).astype(jnp.float32)
        return {'x': x, 'Wq': mk(ks[1]), 'bq': jnp.zeros((D_MODEL,), jnp.float32), 'Wk': mk(ks[2]), 'bk': jnp.zeros((D_MODEL,), jnp.float32), 'Wv': mk(ks[3]), 'bv': jnp.zeros((D_MODEL,), jnp.float32), 'Wo': mk(ks[4]), 'bo': jnp.zeros((D_MODEL,), jnp.float32), 'token_positions': jnp.arange(512, dtype=jnp.int64) if jax.config.jax_enable_x64 else jnp.arange(512, dtype=jnp.int32)}
    _L0_attn_in = _L0_attn_setup()

    def _L0_ffn_setup():
        import jax, jax.numpy as jnp
        import numpy as np
        import math
        BETA = 0.9
        THRESHOLD = 1.0
        NUM_STEPS = 5
        ALPHA = 2.0

        @jax.custom_vjp
        def spike_fn(u):
            return (u > 0).astype(u.dtype)

        def _spike_fwd(u):
            return (spike_fn(u), u)

        def _spike_bwd(u, g):
            s = jnp.pi / 2.0 * ALPHA * u
            return (g * (ALPHA / 2.0) / (1.0 + s * s),)
        spike_fn.defvjp(_spike_fwd, _spike_bwd)
        key = jax.random.key(seed)
        k1, k2, k3 = jax.random.split(key, 3)
        n_embd = 256
        x = jax.random.normal(k1, (4, 512, n_embd), dtype=jnp.float32)
        W_fc = jax.random.normal(k2, (4 * n_embd, n_embd), dtype=jnp.float32) / math.sqrt(n_embd)
        W_proj = jax.random.normal(k3, (n_embd, 4 * n_embd), dtype=jnp.float32) / math.sqrt(4 * n_embd)
        return {'x': x, 'W_fc': W_fc, 'W_proj': W_proj}
    _L0_ffn_in = _L0_ffn_setup()
    _d = {'L0_attn_x': _L0_attn_in['x'], 'L0_attn_Wq': _L0_attn_in['Wq'], 'L0_attn_bq': _L0_attn_in['bq'], 'L0_attn_Wk': _L0_attn_in['Wk'], 'L0_attn_bk': _L0_attn_in['bk'], 'L0_attn_Wv': _L0_attn_in['Wv'], 'L0_attn_bv': _L0_attn_in['bv'], 'L0_attn_Wo': _L0_attn_in['Wo'], 'L0_attn_bo': _L0_attn_in['bo'], 'L0_attn_token_positions': _L0_attn_in['token_positions'], 'L0_ffn_W_fc': _L0_ffn_in['W_fc'], 'L0_ffn_W_proj': _L0_ffn_in['W_proj']}
    _x0 = _d['L0_attn_x']
    _d['L0_attn_x'] = jax.random.normal(jax.random.fold_in(jax.random.key(seed), 1), (16, 1024, 256), dtype=_x0.dtype)
    del _x0
    return _d

def reference(L0_attn_x, L0_attn_Wq, L0_attn_bq, L0_attn_Wk, L0_attn_bk, L0_attn_Wv, L0_attn_bv, L0_attn_Wo, L0_attn_bo, L0_attn_token_positions, L0_ffn_W_fc, L0_ffn_W_proj):

    def _L0_attn_ref(x, Wq, bq, Wk, bk, Wv, bv, Wo, bo, token_positions):
        import jax, jax.numpy as jnp
        import numpy as np
        D_MODEL = 256
        NUM_HEADS = 16
        D_K = D_MODEL // NUM_HEADS
        THETA = 10000.0
        NEG_INF = -1000000000.0

        def _rope(x, positions):
            half = D_K // 2
            inv_freq = 1.0 / THETA ** (jnp.arange(0, D_K, 2, dtype=jnp.float32) / D_K)
            angles = positions.astype(jnp.float32)[:, None] * inv_freq
            cos, sin = (jnp.cos(angles), jnp.sin(angles))
            xe = x[..., 0::2]
            xo = x[..., 1::2]
            re = xe * cos - xo * sin
            ro = xe * sin + xo * cos
            return jnp.stack([re, ro], axis=-1).reshape(x.shape).astype(x.dtype)
        B, S, D = x.shape
        Q = x @ Wq.T + bq
        K = x @ Wk.T + bk
        V = x @ Wv.T + bv

        def split_heads(t):
            return t.reshape(B, S, NUM_HEADS, D_K).transpose(0, 2, 1, 3)
        Q, K, V = (split_heads(Q), split_heads(K), split_heads(V))
        pos = jnp.arange(S)
        Q = _rope(Q, pos)
        K = _rope(K, pos)
        scale = 1.0 / jnp.sqrt(jnp.float32(D_K))
        scores = jnp.einsum('bhqd,bhkd->bhqk', Q, K) * scale
        causal = jnp.tril(jnp.ones((S, S), dtype=bool))
        scores = jnp.where(causal, scores, NEG_INF)
        weights = jax.nn.softmax(scores, axis=-1)
        attn = jnp.einsum('bhqk,bhkd->bhqd', weights, V)
        concat = attn.transpose(0, 2, 1, 3).reshape(B, S, D)
        return concat @ Wo.T + bo

    def _L0_ffn_ref(x, W_fc, W_proj):
        import jax, jax.numpy as jnp
        import numpy as np
        import math
        BETA = 0.9
        THRESHOLD = 1.0
        NUM_STEPS = 5
        ALPHA = 2.0

        @jax.custom_vjp
        def spike_fn(u):
            return (u > 0).astype(u.dtype)

        def _spike_fwd(u):
            return (spike_fn(u), u)

        def _spike_bwd(u, g):
            s = jnp.pi / 2.0 * ALPHA * u
            return (g * (ALPHA / 2.0) / (1.0 + s * s),)
        spike_fn.defvjp(_spike_fwd, _spike_bwd)
        h = jnp.square(jax.nn.relu(jnp.einsum('bsd,fd->bsf', x, W_fc)))
        y = jnp.einsum('bsf,df->bsd', h, W_proj)

        def step(mem, _):
            reset = jax.lax.stop_gradient(spike_fn(mem - THRESHOLD))
            mem_new = BETA * mem + y - reset * THRESHOLD
            spk = spike_fn(mem_new - THRESHOLD)
            return (mem_new, spk)
        mem0 = jnp.zeros_like(y)
        _, spks = jax.lax.scan(step, mem0, None, length=NUM_STEPS)
        return jnp.sum(spks, axis=0) / NUM_STEPS
    x = L0_attn_x
    xn = _layernorm(x, axis=-1)
    x = x + _L0_attn_ref(xn, L0_attn_Wq, L0_attn_bq, L0_attn_Wk, L0_attn_bk, L0_attn_Wv, L0_attn_bv, L0_attn_Wo, L0_attn_bo, L0_attn_token_positions) + _L0_ffn_ref(xn, L0_ffn_W_fc, L0_ffn_W_proj)
    return x

_drawn_inputs = setup_inputs


def setup_inputs(seed=0):
    import zlib

    import numpy as np

    out = dict(_drawn_inputs(seed))
    spreads = {'L0_attn_bq': (0.0, 0.8),
     'L0_attn_bk': (0.0, 0.8),
     'L0_attn_bv': (0.0, 0.1),
     'L0_attn_bo': (0.0, 0.1)}
    factors = {}
    for name, (base, spread) in spreads.items():
        noise = np.random.default_rng([zlib.crc32(name.encode()), seed]).standard_normal(out[name].shape)
        drawn = base * np.exp(spread * noise) if base else spread * noise
        out[name] = jnp.asarray(drawn.astype(out[name].dtype))
    for name, factor in factors.items():
        out[name] = (out[name] * factor).astype(out[name].dtype)
    return out
```

```python
from contextlib import ExitStack

import numpy as np
import concourse.bass as bass
from concourse import mybir

F32, F32R, BF16, I32 = mybir.dt.float32, mybir.dt.float32r, mybir.dt.bfloat16, mybir.dt.int32
ALU, ACT, AX = mybir.AluOpType, mybir.ActivationFunctionType, mybir.AxisListType

P = 128
B, S, D = 16, 1024, 256
H, DK, F = 16, 16, 1024
NF = DK // 2
THETA, LN_EPS, SCALE = 10000.0, 1e-5, 1.0 / DK ** 0.5
BETA, THRESHOLD, STEPS = 0.9, 1.0, 5
NT = S // P
G = 512
NG = S // G
KD = D // P
NFT = F // P
NTILE = H // 2
NQUAD = H // 4
VW = DK + 1
BOUND_HALF = 131 / 256
GAP_LIMIT = 64.0 / SCALE
MASKED = -1e30

UNITS = [(kt, g) for kt in range(NT) for g in range(NG) if (g + 1) * G > kt * P]
NU = len(UNITS)
NUNIT = NQUAD * NU
DIAG = [kt // (G // P) == g for kt, g in UNITS]
ND = sum(DIAG)
LAG = 2
NPB = 4
NSLOT = 3


def first_query(kt, g):
    return max(kt * P, g * G)


def diag_before(n):
    return n // NU * ND + sum(DIAG[:n % NU])


def spike_thresholds():
    f = np.float32

    def count(y):
        mem, spikes = f(0), 0
        for _ in range(STEPS):
            reset = f(mem - f(THRESHOLD) > 0)
            mem = f(f(f(BETA) * mem + y) - reset * f(THRESHOLD))
            spikes += bool(mem - f(THRESHOLD) > 0)
        return spikes

    edges = []
    for n in range(1, STEPS + 1):
        lo, hi = f(0), f(2)
        while np.nextafter(lo, hi) < hi:
            mid = f((lo + hi) / f(2))
            mid = mid if lo < mid < hi else np.nextafter(lo, hi)
            lo, hi = (lo, mid) if count(mid) >= n else (mid, hi)
        edges.append(float(lo))
    return edges


def layer_kernel(nc, x, wqk, bqk, wv, bv, wfc, wproj, wo, bo, tables, consts, out):
    edges = spike_thresholds()
    with ExitStack() as ctx:
        arena_at = (nc.sbuf_base + 31) // 32 * 32
        ctx.enter_context(nc.sbuf_tensor("arena", [P, 8192], F32))

        def shared(name, shape, dt, at):
            return nc.alloc_sbuf_tensor_at(name, shape, dt, offset=arena_at + at)

        def sb(name, shape, dt=F32):
            return ctx.enter_context(nc.sbuf_tensor(name, shape, dt))

        KB = 1024
        probs = [shared(f"probs{i}", [P, 4, G], F32, 8 * KB * i) for i in range(NPB)]
        planes = [shared(f"planes{i}", [P, 2, 2, G], F32R, 8 * KB * i) for i in range(2)]
        rot_a = shared("rot_a", [P, 2, G], F32, 16 * KB)
        rot_b = shared("rot_b", [P, 2, G], F32, 20 * KB)
        rot = [shared(f"rot{i}", [P, 2, G], F32, (24 + 4 * i) * KB) for i in range(2)]
        h_hi = [shared(f"h_hi{i}", [P, G], F32R, 2 * KB * i) for i in range(3)]
        h_lo = [shared(f"h_lo{i}", [P, G], F32R, (6 + 2 * i) * KB) for i in range(3)]
        relu = [shared(f"relu{i}", [P, G], F32, (16 + 2 * i) * KB) for i in range(2)]
        h_sq = [shared(f"h_sq{i}", [P, G], F32, (20 + 2 * i) * KB) for i in range(2)]
        count = shared("count", [P, 2, G], F32, 28 * KB)
        wqk_in = shared("wqk_in", [P, KD, 4 * P], F32, 0)
        wv_in = shared("wv_in", [P, KD, D], F32, 4 * KB)
        wfc_in = shared("wfc_in", [P, KD, F], F32, 8 * KB)
        wproj_in = shared("wproj_in", [P, NFT, D], F32, 16 * KB)

        xn_at = (nc.sbuf_base + 31) // 32 * 32
        xn = sb("xn", [P, NT, D])
        squares = nc.alloc_sbuf_tensor_at("squares", [P, 4, 2, G], BF16, offset=xn_at)

        q_stack = sb("q_stack", [P, NTILE, S], F32R)
        k_stack = sb("k_stack", [P, NTILE, S], F32R)
        wqk_hi, wqk_lo = sb("wqk_hi", [P, KD, 4 * P], F32R), sb("wqk_lo", [P, KD, 4 * P], F32R)
        wv_hi, wv_lo = sb("wv_hi", [P, KD, D], F32R), sb("wv_lo", [P, KD, D], F32R)
        wfc_hi, wfc_lo = sb("wfc_hi", [P, KD, F], F32R), sb("wfc_lo", [P, KD, F], F32R)
        wproj_hi, wproj_lo = sb("wproj_hi", [P, NFT, D], F32R), sb("wproj_lo", [P, NFT, D], F32R)
        wo_sb = sb("wo_sb", [P, KD, D])
        table = sb("table", [P, 2, S])
        xT_hi, xT_lo = sb("xT_hi", [P, KD, S], F32R), sb("xT_lo", [P, KD, S], F32R)
        v_sb = sb("v_sb", [P, NT, H, VW])
        x_sb = sb("x_sb", [P, NT, D])
        resid = sb("resid", [P, NT, D])
        attn = sb("attn", [P, KD, S])
        numer_at = (nc.sbuf_base + 31) // 32 * 32
        numer = sb("numer", [P, S])
        shift = nc.alloc_sbuf_tensor_at("shift", [64, S], F32R, offset=numer_at)
        own_qk = nc.alloc_sbuf_tensor_at("own_qk", [P, NG, 2, G], BF16, offset=numer_at)
        denom = sb("denom", [64, P])
        recip_at = (nc.sbuf_base + 31) // 32 * 32
        recip_rows = sb("recip_rows", [P, S])
        out_sb = [nc.alloc_sbuf_tensor_at(f"out_sb{i}", [P, 2, D], F32, offset=recip_at + 2 * KB * i) for i in range(2)]
        const = sb("const", [P, 2 * P + 3 * H])
        ident, causal = const[:, 0:P], const[:, P:2 * P]
        sel = sb("sel", [P, 3, H], BF16)
        bqk_sb, neg_bqk = sb("bqk_sb", [P, 4]), sb("neg_bqk", [P, 4])
        bv_sb, bo_sb = sb("bv_sb", [P, D]), sb("bo_sb", [P, D])
        stats = sb("stats", [P, NT, 6])
        mean, var, mean_gap, rstd = (sb(n, [P, NT]) for n in ("mean", "var", "mean_gap", "rstd"))
        ln_a, ln_b, neg_half = (sb(n, [P, NT]) for n in ("ln_a", "ln_b", "neg_half"))
        k_max, q_gap, gap, gap_all = (sb(n, [H, 1]) for n in ("k_max", "q_gap", "gap", "gap_all"))
        flag = sb("flag", [1, 1], I32)
        row_max = sb("row_max", [P, NT, H])

        recip_dram = nc.dram_tensor("recip_dram", [KD, H // KD, S], F32, kind="Internal").ap()

        pair = [ctx.enter_context(nc.psum_tensor(f"pair{i}", [P, 2, G], F32)) for i in range(4)]
        OPAIR = 3

        def sem(name):
            return ctx.enter_context(nc.semaphore(name))

        w_in, w_split, consts_in, cleared = sem("w_in"), sem("w_split"), sem("consts_in"), sem("cleared")
        x_in = sem("x_in")
        stats_done, var_done = sem("stats_done"), sem("var_done")
        ln_step, vec_step = sem("ln_step"), sem("vec_step")
        rstd_done, xn_done, xb_done = sem("rstd_done"), sem("xn_done"), sem("xb_done")
        xT_ps, xT_hi_done, xT_lo_done = sem("xT_ps"), sem("xT_hi_done"), sem("xT_lo_done")
        qk_ps, rot_done, rot_sum = sem("qk_ps"), sem("rot_done"), sem("rot_sum")
        plane_hi, plane_lo, sq_done = sem("plane_hi"), sem("plane_lo"), sem("sq_done")
        stacked = [sem("stacked0"), sem("stacked1")]
        v_ps, v_done = sem("v_ps"), sem("v_done")
        wo_ps, out_done = sem("wo_ps"), sem("out_done")
        out_sent = [sem("out_sent0"), sem("out_sent1")]
        own_done, norm_ps, norm_used, gap_done, gap_max, flag_done = (
            sem(n) for n in ("own_done", "norm_ps", "norm_used", "gap_done", "gap_max", "flag_done"))
        max_ps, max_done, max_step = sem("max_ps"), sem("max_done"), sem("max_step")
        shift_done, shift_in = sem("shift_done"), sem("shift_in")
        fc_ps, relu_done, sq_h = sem("fc_ps"), sem("relu_done"), sem("sq_h")
        h_hi_done, h_lo_done, proj_done = sem("h_hi_done"), sem("h_lo_done"), sem("proj_done")
        spike_step, resid_done = sem("spike_step"), sem("resid_done")
        scores_ps, exp_done, mask_done, pv_done = (
            sem(n) for n in ("scores_ps", "exp_done", "mask_done", "pv_done"))
        numer_done = sem("numer_done")
        numer_in = [sem("numer_in0"), sem("numer_in1")]
        denom_in, recip_done = sem("denom_in"), sem("recip_done")
        recip_out, recip_in, attn_done = sem("recip_out"), sem("recip_in"), sem("attn_done")
        NMAX = H * NT
        NFC = NG * NFT
        STACK_DMAS = 2 * 3 * 2
        NSPIKE = 2 * STEPS

        stood = sem("stood")

        def alone(eng, s, value):
            eng.wait_ge(s, value)
            eng.sem_inc(stood, 1)

        block = ctx.enter_context(nc.Block())

        @block.sync
        def _(sp):
            for dst, src in ((wqk_in, wqk), (wv_in, wv), (wfc_in, wfc), (wproj_in, wproj)):
                sp.dma_start(dst[:, :, :], src.rearrange("(k p) n -> p k n", p=P)).then_inc(w_in, 16)
            sp.dma_start(const[:, :], consts).then_inc(consts_in, 16)
            sp.dma_start(wo_sb[:, :, :], wo.rearrange("(k p) n -> p k n", p=P)).then_inc(consts_in, 16)
            sp.dma_start(table[:, :, :], tables.rearrange("t p s -> p t s")).then_inc(consts_in, 16)
            sp.dma_start(bqk_sb[:, :], bqk).then_inc(consts_in, 16)
            sp.dma_start(bv_sb[:, :], bv.partition_broadcast(P)).then_inc(consts_in, 16)
            sp.dma_start(bo_sb[:, :], bo.partition_broadcast(P)).then_inc(consts_in, 16)

            def load_x(b, wait):
                if wait is not None:
                    alone(sp, resid_done, wait * NG + NG)
                sp.dma_start(x_sb[:, :, :], x[b].rearrange("(t p) d -> p t d", p=P)).then_inc(x_in, 16)

            def stack(b):
                for u in range(4):
                    g, is_k = u // 2, u % 2
                    dst = k_stack if is_k else q_stack
                    buf = planes[u % 2]
                    sp.wait_ge(plane_hi, b * 4 + u + 1)
                    sp.wait_ge(plane_lo, b * 4 + u + 1)
                    for half in range(2):
                        for part in range(3):
                            lo = part == (1 if is_k else 2)
                            for eo in range(2):
                                row = 64 * half + 16 * part + 8 * eo
                                sp.dma_start(dst[row:row + NF, :, g * G:(g + 1) * G].bitcast(F32),
                                             buf[64 * half:64 * half + 64, int(lo), eo, :].bitcast(F32)
                                             ).then_inc(stacked[u % 2], 16)

            def store(b):
                for n in range(4):
                    alone(sp, out_done, b * 4 + n + 1)
                    sp.dma_start(out[b].rearrange("(t p) d -> p t d", p=P)[:, 2 * n:2 * n + 2, :],
                                 out_sb[n % 2][:, :, :]).then_inc(out_sent[n % 2], 16)
                for s in out_sent:
                    alone(sp, s, (b + 1) * 2 * 16)

            def load_shift(b):
                sp.wait_ge(shift_done, b + 1)
                for half in range(2):
                    for lo in range(2):
                        row = 64 * half + 48 + lo
                        src = 32 * lo + 8 * half
                        sp.dma_start(q_stack[row:row + 1, :, :].bitcast(F32), shift[src:src + 8, :].bitcast(F32)
                                     ).then_inc(shift_in, 16)

            def gather(b):
                for quad in range(NQUAD):
                    k, base = quad // 2, quad % 2 * 64
                    sp.wait_ge(numer_done, (b * NQUAD + quad) * 2 + 2)
                    sp.dma_start(denom[base // 2:base // 2 + 32, :], numer[DK:P:32, :]).then_inc(denom_in, 16)
                    for i in range(4):
                        sp.dma_start(attn[base + DK * i:base + DK * (i + 1), k, :],
                                     numer[32 * i:32 * i + DK, :]).then_inc(numer_in[k], 16)
                    if quad % 2:
                        sp.wait_ge(recip_done, b * KD + k + 1)
                        sp.dma_start(recip_dram[k].rearrange("h (c q) -> (h c) q", q=P), denom[:, :]
                                     ).then_inc(recip_out, 16)
                        alone(sp, recip_out, (b * KD + k + 1) * 16)
                        sp.dma_start(recip_rows[:, :],
                                     recip_dram[k].unsqueeze(1).broadcast_to([H // KD, DK, S])
                                     ).then_inc(recip_in, 16)

            def attention(b, more):
                if more:
                    load_x(b + 1, b)
                gather(b)

            load_x(0, None)
            stack(0)
            load_shift(0)
            with sp.Fori(0, B - 1) as b:
                attention(b, True)
                stack(b + 1)
                store(b)
                load_shift(b + 1)
            attention(B - 1, False)
            store(B - 1)

        @block.gpsimd
        def _(pool):
            def chained(ins):
                ins.then_inc(ln_step, 1)

            pool.memset(v_sb[:, :, :, DK:VW], 1.0).then_inc(cleared, 1)
            pool.memset(neg_half[:, :], -0.5).then_inc(ln_step, 1)
            pool.memset(q_stack[:, :, :].bitcast(F32), 0.0).then_inc(cleared, 1)
            pool.wait_ge(ln_step, 1)
            LN_OPS = 5

            def root(b):
                base = b * LN_OPS + 1
                pool.wait_ge(var_done, b + 1)
                chained(pool.tensor_tensor(ln_a[:, :], var[:, :], neg_half[:, :], ALU.pow))
                pool.wait_ge(ln_step, base + 1)
                chained(pool.tensor_tensor(ln_b[:, :], ln_a[:, :], ln_a[:, :], ALU.mult))
                pool.wait_ge(ln_step, base + 2)
                chained(pool.tensor_tensor(ln_b[:, :], ln_b[:, :], var[:, :], ALU.mult))
                alone(pool, ln_step, base + 3)
                chained(pool.tensor_scalar(ln_b[:, :], ln_b[:, :], -0.5, 1.5, ALU.mult, ALU.add))
                pool.wait_ge(ln_step, base + 4)
                chained(pool.tensor_tensor(ln_b[:, :], ln_b[:, :], ln_a[:, :], ALU.mult))
                alone(pool, ln_step, base + 5)
                pool.tensor_copy(rstd[:, :], ln_b[:, :]).then_inc(rstd_done, 1)

            def add_bo(b):
                pool.wait_ge(xn_done, b * NT + NT)
                for t in range(NT):
                    ins = pool.tensor_tensor(x_sb[:, t, :], x_sb[:, t, :], bo_sb[:, :], ALU.add)
                ins.then_inc(xb_done, 1)

            def rotary(b, last):
                for u in range(4):
                    pool.wait_ge(rot_done, b * 4 + u + 1)
                    if u >= 2:
                        pool.wait_ge(sq_done, b * 4 + u - 1)
                        pool.wait_ge(plane_lo, b * 4 + u - 1)
                        pool.wait_ge(own_done, b * NG + 1)
                    pool.tensor_tensor(rot[u % 2][:, :, :], rot_a[:, :, :], rot_b[:, :, :], ALU.add
                                       ).then_inc(rot_sum, 1)
                    if u % 2:
                        if u == 1 and last is not None:
                            pool.wait_ge(numer_in[1], (last + 1) * 2 * 4 * 16)
                            pool.wait_ge(denom_in, (last + 1) * NQUAD * 16)
                        pool.wait_ge(rot_sum, b * 4 + u + 1)
                        pool.tensor_tensor(own_qk[:, u // 2, :, :], rot[0][:, :, :], rot[1][:, :, :], ALU.mult
                                           ).then_inc(own_done, 1)

            def widest_gap(b):
                alone(pool, gap_done, b + 1)
                pool.partition_all_reduce(gap_all[:, :], gap[:, :], H, bass.bass_isa.ReduceOp.max
                                          ).then_inc(gap_max, 1)

            def h_low(b):
                for i in range(NFC):
                    if i == 0:
                        for s in stacked:
                            pool.wait_ge(s, (b + 1) * 2 * STACK_DMAS * 16)
                    if i >= 3:
                        pool.wait_ge(proj_done, b * NFC + i - 2)
                    pool.wait_ge(h_hi_done, b * NFC + i + 1)
                    pool.tensor_tensor(h_lo[i % 3][:, :], h_sq[i % 2][:, :], h_hi[i % 3][:, :].bitcast(F32),
                                       ALU.subtract).then_inc(h_lo_done, 1)

            def mask(b, quads):
                for n in (q * NU + i for q in quads for i in range(NU) if DIAG[i]):
                    alone(pool, exp_done, (b * NUNIT + n) * 2 + 2)
                    view = probs[n % NPB][:, :, 0:P]
                    pool.affine_select(view, view, [[0, 4], [1, P]], ALU.is_ge, 0.0, base=0,
                                       channel_multiplier=-1).then_inc(mask_done, 1)

            def dense(b, last):
                rotary(b, last)
                widest_gap(b)
                h_low(b)

            pool.wait_ge(consts_in, 16 * 6)
            root(0)
            add_bo(0)
            dense(0, None)
            with pool.Fori(0, B - 1) as b:
                mask(b, [0])
                root(b + 1)
                mask(b, [1])
                add_bo(b + 1)
                mask(b, [2, 3])
                dense(b + 1, b)
            mask(B - 1, range(NQUAD))

        @block.scalar
        def _(act):
            def high_xT(b):
                for n in range(4):
                    g, k = n // 2, n % 2
                    act.wait_ge(xT_ps, b * 4 + n + 1)
                    act.activation(xT_hi[:, k, g * G:(g + 1) * G], pair[k][:, g, :], ACT.Copy
                                   ).then_inc(xT_hi_done, 1)

            def high_qk(b):
                for u in range(4):
                    act.wait_ge(rot_sum, b * 4 + u + 1)
                    if u >= 2:
                        act.wait_ge(stacked[u % 2], (b * 2 + 1) * STACK_DMAS * 16)
                    act.activation(planes[u % 2][:, 0, :, :], rot[u % 2][:, :, :], ACT.Copy).then_inc(plane_hi, 1)
                    act.activation(squares[:, u, :, :], rot[u % 2][:, :, :], ACT.Square).then_inc(sq_done, 1)

            def activate_h(b):
                def rectify(i):
                    if i == 0:
                        act.wait_ge(rot_sum, b * 4 + 4)
                    act.wait_ge(fc_ps, b * NFC + i + 1)
                    act.activation(relu[i % 2][:, :], pair[i // 2 % 2][:, i % 2, :], ACT.Relu).then_inc(relu_done, 1)

                rectify(0)
                for i in range(NFC):
                    if i + 1 < NFC:
                        if i >= 1:
                            act.wait_ge(sq_h, b * NFC + i)
                        rectify(i + 1)
                    if i >= 2:
                        act.wait_ge(h_lo_done, b * NFC + i - 1)
                    act.wait_ge(relu_done, b * NFC + i + 1)
                    act.activation(h_sq[i % 2][:, :], relu[i % 2][:, :], ACT.Square).then_inc(sq_h, 1)

            def exponentials(b):
                for n in range(NUNIT):
                    kt, g = UNITS[n % NU]
                    w = (g + 1) * G - first_query(kt, g)
                    if n >= NPB:
                        act.wait_ge(pv_done, b * NUNIT + n - NPB + 1)
                    if n == NPB - 1:
                        act.wait_ge(resid_done, b * NG + NG)
                    for pr in range(2):
                        m = 2 * n + pr
                        act.wait_ge(scores_ps, b * 2 * NUNIT + m + 1)
                        act.activation(probs[n % NPB][:, 2 * pr:2 * pr + 2, 0:w], pair[m % NSLOT][:, :, 0:w],
                                       ACT.Exp, scale=SCALE).then_inc(exp_done, 1)

            def dense(b):
                high_xT(b)
                high_qk(b)
                activate_h(b)

            act.wait_ge(w_split, 9)
            dense(0)
            with act.Fori(0, B - 1) as b:
                exponentials(b)
                dense(b + 1)
            exponentials(B - 1)

        @block.vector
        def _(dve):
            dve.memset(k_stack[:, :, :].bitcast(F32), 1.0).then_inc(cleared, 1)
            dve.wait_ge(w_in, 16 * 4)
            for hi, lo, whole in ((wqk_hi, wqk_lo, wqk_in), (wv_hi, wv_lo, wv_in), (wfc_hi, wfc_lo, wfc_in),
                                  (wproj_hi, wproj_lo, wproj_in)):
                dve.tensor_copy(hi[:, :, :], whole[:, :, :]).then_inc(w_split, 1)
            for n, (hi, lo, whole) in enumerate(((wqk_hi, wqk_lo, wqk_in), (wv_hi, wv_lo, wv_in),
                                                 (wfc_hi, wfc_lo, wfc_in), (wproj_hi, wproj_lo, wproj_in))):
                dve.wait_ge(w_split, 4 + n)
                dve.tensor_tensor(lo[:, :, :], whole[:, :, :], hi[:, :, :].bitcast(F32), ALU.subtract
                                  ).then_inc(w_split, 1)
            dve.wait_ge(consts_in, 16 * 6)
            dve.tensor_copy(sel[:, :, :].rearrange("p a h -> p (a h)"), const[:, 2 * P:2 * P + 3 * H]).then_inc(vec_step, 1)
            dve.tensor_scalar(neg_bqk[:, :], bqk_sb[:, :], -1.0, None, ALU.mult).then_inc(w_split, 1)
            dve.wait_ge(w_split, 9)

            def statistics(b):
                base = b * 6 + 1
                dve.wait_ge(x_in, b * 16 + 16)
                for t in range(NT):
                    dve.bn_stats(stats[:, t, :], x_sb[:, t, :]).then_inc(stats_done, 1)
                dve.wait_ge(stats_done, b * NT + NT)
                dve.tensor_tensor(mean_gap[:, :], stats[:, :, 1], stats[:, :, 4], ALU.subtract).then_inc(vec_step, 1)
                dve.tensor_tensor(mean[:, :], stats[:, :, 1], stats[:, :, 4], ALU.add).then_inc(vec_step, 1)
                dve.tensor_tensor(var[:, :], stats[:, :, 2], stats[:, :, 5], ALU.add).then_inc(vec_step, 1)
                dve.wait_ge(vec_step, base + 3)
                dve.tensor_tensor(mean_gap[:, :], mean_gap[:, :], mean_gap[:, :], ALU.mult).then_inc(vec_step, 1)
                dve.tensor_scalar(mean[:, :], mean[:, :], 0.5, None, ALU.mult).then_inc(vec_step, 1)
                dve.tensor_scalar(var[:, :], var[:, :], 1.0 / D, LN_EPS, ALU.mult, ALU.add).then_inc(vec_step, 1)
                dve.wait_ge(vec_step, base + 6)
                dve.scalar_tensor_tensor(var[:, :], mean_gap[:, :], 0.25, var[:, :], ALU.mult, ALU.add
                                         ).then_inc(var_done, 1)

            def normalise(b):
                dve.wait_ge(rstd_done, b + 1)
                for t in range(NT):
                    dve.tensor_scalar(xn[:, t, :], x_sb[:, t, :], mean[:, t:t + 1], rstd[:, t:t + 1],
                                      ALU.subtract, ALU.mult).then_inc(xn_done, 1)

            def low_xT(b):
                for n in range(4):
                    g, k = n // 2, n % 2
                    cols = slice(g * G, (g + 1) * G)
                    dve.wait_ge(xT_hi_done, b * 4 + n + 1)
                    dve.tensor_tensor(xT_lo[:, k, cols], pair[k][:, g, :], xT_hi[:, k, cols].bitcast(F32),
                                      ALU.subtract).then_inc(xT_lo_done, 1)

            def qk_pair(u):
                return (2, 3, 0, 1)[u]

            def rotate(b, u):
                g, is_k = u // 2, u % 2
                cos, sin = (table[:, n, g * G:(g + 1) * G] for n in range(2))
                even, odd = (pair[qk_pair(u)][:, eo, :] for eo in range(2))
                e_bias, o_bias = (bqk_sb[:, 2 * is_k + eo:2 * is_k + eo + 1] for eo in range(2))
                neg_o_bias = neg_bqk[:, 2 * is_k + 1:2 * is_k + 2]
                dve.wait_ge(qk_ps, b * 4 + u + 1)
                if u >= 1:
                    dve.wait_ge(rot_sum, b * 4 + u)
                dve.scalar_tensor_tensor(rot_a[:, 0, :], even, e_bias, cos, ALU.add, ALU.mult)
                dve.scalar_tensor_tensor(rot_a[:, 1, :], even, e_bias, sin, ALU.add, ALU.mult)
                dve.scalar_tensor_tensor(rot_b[:, 0, :], odd, neg_o_bias, sin, ALU.subtract, ALU.mult, reverse0=True)
                dve.scalar_tensor_tensor(rot_b[:, 1, :], odd, o_bias, cos, ALU.add, ALU.mult).then_inc(rot_done, 1)

            def low_qk(b, u):
                dve.wait_ge(plane_hi, b * 4 + u + 1)
                dve.tensor_tensor(planes[u % 2][:, 1, :, :], rot[u % 2][:, :, :],
                                  planes[u % 2][:, 0, :, :].bitcast(F32), ALU.subtract).then_inc(plane_lo, 1)

            def take_v(b):
                for t in range(NT):
                    n = t // 2
                    if t % 2 == 0:
                        dve.wait_ge(v_ps, b * 4 + n + 1)
                    heads = pair[2 + n // 2][:, n % 2, (t % 2) * D:(t % 2 + 1) * D]
                    dve.tensor_tensor(v_sb[:, t, :, 0:DK], heads.rearrange("p (h d) -> p h d", d=DK),
                                      bv_sb[:, :].rearrange("p (h d) -> p h d", d=DK), ALU.add).then_inc(v_done, 1)

            def invert(b, k):
                dve.wait_ge(denom_in, (b * NQUAD + 2 * k + 2) * 16)
                dve.reciprocal(denom[:, :], denom[:, :]).then_inc(recip_done, 1)

            def divide(b, k):
                dve.wait_ge(numer_in[k], (b + 1) * 2 * 4 * 16)
                dve.wait_ge(recip_in, (b * KD + k + 1) * 16)
                dve.tensor_tensor(attn[:, k, :], attn[:, k, :], recip_rows[:, :], ALU.mult).then_inc(attn_done, 1)

            def finish(b):
                for n in range(4):
                    if n >= 2:
                        dve.wait_ge(out_sent[n % 2], (b * 2 + 1) * 16)
                    dve.wait_ge(wo_ps, b * 4 + n + 1)
                    dve.tensor_tensor(out_sb[n % 2][:, :, :], pair[n // 2][:, n % 2, :].rearrange(
                        "p (t d) -> p t d", d=D), resid[:, 2 * n:2 * n + 2, :], ALU.add).then_inc(out_done, 1)

            def bound(b):
                dve.wait_ge(norm_ps, b + 1)
                dve.tensor_reduce(k_max[:, :], pair[3][0:H, :, :], AX.XY, ALU.max).then_inc(norm_used, 1)
                dve.tensor_reduce(q_gap[:, :], pair[2][32:32 + H, :, :], AX.XY, ALU.max).then_inc(norm_used, 1)
                dve.wait_ge(norm_used, b * 3 + 2)
                dve.scalar_tensor_tensor(gap[:, :], k_max[:, :], BOUND_HALF, q_gap[:, :], ALU.mult, ALU.add
                                         ).then_inc(gap_done, 1)
                dve.tensor_scalar(shift[0:H, :].rearrange("h (g q) -> h g q", q=G), pair[2][0:H, :, :],
                                  k_max[:, 0:1], -BOUND_HALF, ALU.add, ALU.mult).then_inc(norm_used, 1)

            def raise_flag(b):
                dve.wait_ge(gap_max, b + 1)
                dve.tensor_scalar(flag[:, :], gap_all[0:1, :], GAP_LIMIT, None, ALU.is_gt).then_inc(flag_done, 1)

            def exact_shift(b):
                flat = pair[1][:, :, :].rearrange("p a q -> p (a q)")
                for m in range(NMAX):
                    h, qt = m // NT, m % NT
                    col = (h % 2) * 8 + h // 2
                    dve.wait_ge(max_ps, b * (NMAX + 1) + m + 1)
                    dve.tensor_tensor(flat[:, qt * P:(qt + 1) * P], flat[:, qt * P:(qt + 1) * P], causal, ALU.add
                                      ).then_inc(max_step, 1)
                    dve.wait_ge(max_step, b * (NMAX + 1) + m + 1)
                    dve.tensor_reduce(row_max[:, qt, col:col + 1], flat[:, 0:(qt + 1) * P], AX.X, ALU.max
                                      ).then_inc(max_done, 1)
                dve.wait_ge(max_ps, b * (NMAX + 1) + NMAX + 1)
                heads = pair[3][0:H, :, :].rearrange("p a q -> p (a q)")
                dve.tensor_scalar(shift[0:H, :], heads, -1.0, None, ALU.mult).then_inc(max_step, 1)
                dve.wait_ge(max_step, b * (NMAX + 1) + NMAX + 1)
                dve.scalar_tensor_tensor(shift[32:32 + H, :], heads, -1.0, shift[0:H, :].bitcast(F32),
                                         ALU.mult, ALU.subtract).then_inc(shift_done, 1)

            def settle_shift(b):
                dve.wait_ge(flag_done, b + 1)
                dve.memset(row_max[:, :, :], 0.0)
                loose = dve.value_load(flag[0:1, 0:1], min_val=0, max_val=1)
                with dve.If(loose > 0):
                    exact_shift(b)
                with dve.Else():
                    dve.sem_inc(max_done, NMAX)
                    dve.sem_inc(max_step, NMAX + 1)
                    dve.memset(shift[32:32 + H, :].bitcast(F32), 0.0).then_inc(shift_done, 1)

            def high_h(b, i):
                if i == 0:
                    for s in stacked:
                        dve.wait_ge(s, (b + 1) * 2 * STACK_DMAS * 16)
                if i >= 3:
                    dve.wait_ge(proj_done, b * NFC + i - 2)
                dve.wait_ge(sq_h, b * NFC + i + 1)
                dve.tensor_copy(h_hi[i % 3][:, :], h_sq[i % 2][:, :]).then_inc(h_hi_done, 1)

            def spikes(b, g, steps):
                base = (b * NG + g) * NSPIKE
                y = pair[2 + g]
                for s in steps:
                    if s == 0:
                        dve.wait_ge(proj_done, b * NFC + (g + 1) * NFT)
                    if s < STEPS:
                        for a in range(2):
                            if s == 0:
                                dve.tensor_scalar(count[:, a, :], y[:, a, :], edges[s], None, ALU.is_gt
                                                  ).then_inc(spike_step, 1)
                            else:
                                dve.wait_ge(spike_step, base + 2 * s + a - 1)
                                dve.scalar_tensor_tensor(count[:, a, :], y[:, a, :], edges[s], count[:, a, :],
                                                         ALU.is_gt, ALU.add).then_inc(spike_step, 1)
                    else:
                        if g == 0:
                            dve.wait_ge(xb_done, b + 1)
                        dve.wait_ge(spike_step, base + NSPIKE)
                        tiles = slice(4 * g, 4 * g + 4)
                        dve.scalar_tensor_tensor(
                            resid[:, tiles, :], count[:, :, :].rearrange("p a (t d) -> p (a t) d", d=D),
                            1.0 / STEPS, x_sb[:, tiles, :], ALU.mult, ALU.add).then_inc(resid_done, 1)

            def project(b, last):
                low_xT(b)
                rotate(b, 0)
                if last is not None:
                    invert(last, 1)
                rotate(b, 1)
                low_qk(b, 0)
                rotate(b, 2)
                low_qk(b, 1)
                if last is not None:
                    divide(last, 1)
                rotate(b, 3)
                low_qk(b, 2)
                take_v(b)
                low_qk(b, 3)

            def mlp(b):
                bound(b)
                for i in range(NFC):
                    high_h(b, i)
                    if i == 4:
                        raise_flag(b)
                    if i == NFT:
                        settle_shift(b)
                    if i >= NFT + 1 and i - NFT - 1 <= STEPS:
                        spikes(b, 0, [i - NFT - 1])
                spikes(b, 1, range(STEPS + 1))

            def attention(b, more):
                if more:
                    statistics(b + 1)
                for quad in range(NQUAD):
                    for g in range(NG):
                        unit = quad * NU + max(n for n in range(NU) if UNITS[n][1] == g)
                        dve.wait_ge(pv_done, b * NUNIT + unit + 1)
                        if g == 0:
                            before = (b * NQUAD + quad)
                            if quad >= 1:
                                k = (quad - 1) // 2
                                dve.wait_ge(numer_in[k], (b * 2 + (quad - 1) % 2 + 1) * 4 * 16)
                                dve.wait_ge(denom_in, before * 16)
                        dve.tensor_copy(numer[:, g * G:(g + 1) * G], pair[OPAIR][:, g, :]).then_inc(numer_done, 1)
                    if quad == 0 and more:
                        normalise(b + 1)
                    if quad == 2:
                        invert(b, 0)
                    if quad == 3:
                        divide(b, 0)

            statistics(0)
            normalise(0)
            project(0, None)
            mlp(0)
            with dve.Fori(0, B - 1) as b:
                attention(b, True)
                project(b + 1, b)
                finish(b)
                mlp(b + 1)
            attention(B - 1, False)
            invert(B - 1, 1)
            divide(B - 1, 1)
            finish(B - 1)

        @block.tensor
        def _(pe):
            def split_product(bank, parts, start=True, last=None):
                for n, (lhsT, rhs) in enumerate(parts):
                    ins = pe.matmul(bank, lhsT, rhs, start=start and n == 0, stop=n == len(parts) - 1)
                return ins

            def transposes(b):
                for n in range(4):
                    g, k = n // 2, n % 2
                    pe.wait_ge(xn_done, b * NT + 4 * g + 4)
                    for t in range(4):
                        ins = pe.transpose(pair[k][:, g, t * P:(t + 1) * P], xn[:, 4 * g + t, k * P:(k + 1) * P], ident)
                    ins.then_inc(xT_ps, 1)

            def queries_keys(b, last):
                for u in range(4):
                    g, is_k = u // 2, u % 2
                    cols = slice(g * G, (g + 1) * G)
                    pe.wait_ge(xT_lo_done, b * 4 + (2 if u < 2 else 4))
                    if u == 1 and last is not None:
                        pe.wait_ge(numer_done, (last + 1) * NQUAD * 2)
                    for eo in range(2):
                        m = slice((2 * is_k + eo) * P, (2 * is_k + eo + 1) * P)
                        parts = [p for k in range(KD) for p in (
                            (wqk_hi[:, k, m], xT_hi[:, k, cols]), (wqk_lo[:, k, m], xT_hi[:, k, cols]),
                            (wqk_hi[:, k, m], xT_lo[:, k, cols]))]
                        ins = split_product(pair[(2, 3, 0, 1)[u]][:, eo, :], parts)
                    ins.then_inc(qk_ps, 1)

            def values(b):
                for t in range(NT):
                    n = t // 2
                    cols = slice(t * P, (t + 1) * P)
                    if t % 4 == 0:
                        pe.wait_ge(rot_done, b * 4 + n // 2 + 1)
                    parts = [p for k in range(KD) for p in (
                        (xT_hi[:, k, cols], wv_hi[:, k, :]), (xT_hi[:, k, cols], wv_lo[:, k, :]),
                        (xT_lo[:, k, cols], wv_hi[:, k, :]))]
                    ins = split_product(pair[2 + n // 2][:, n % 2, (t % 2) * D:(t % 2 + 1) * D], parts)
                    if t % 2:
                        ins.then_inc(v_ps, 1)

            def output(b, next_b):
                pe.wait_ge(attn_done, b * KD + KD)
                for t in range(NT):
                    n = t // 2
                    if next_b is not None and t % 4 == 0:
                        pe.wait_ge(rot_done, next_b * 4 + 3 + n // 2)
                    ins = split_product(pair[n // 2][:, n % 2, (t % 2) * D:(t % 2 + 1) * D],
                                        [(attn[:, k, t * P:(t + 1) * P], wo_sb[:, k, :]) for k in range(KD)])
                    if t % 2:
                        ins.then_inc(wo_ps, 1)

            def norms(b):
                pe.wait_ge(v_done, b * NT + NT)
                pe.wait_ge(sq_done, b * 4 + 4)
                pe.wait_ge(own_done, b * NG + NG)
                for g in range(NG):
                    q2, k2, own = (lambda eo: squares[:, 2 * g, eo, :], lambda eo: squares[:, 2 * g + 1, eo, :],
                                   lambda eo: own_qk[:, g, eo, :])
                    both = range(2)
                    split_product(pair[2][0:H, g, :], [(sel[:, 0, :], q2(eo)) for eo in both])
                    split_product(pair[3][0:H, g, :], [(sel[:, 0, :], k2(eo)) for eo in both])
                    ins = split_product(pair[2][32:32 + H, g, :], [(sel[:, 1, :], q2(eo)) for eo in both]
                                        + [(sel[:, 2, :], own(eo)) for eo in both])
                ins.then_inc(norm_ps, 1)

            def row_maxima(b):
                flat = pair[1][:, :, :].rearrange("p a q -> p (a q)")
                for m in range(NMAX):
                    h, qt = m // NT, m % NT
                    rows = slice(64 * (h % 2), 64 * (h % 2) + 48)
                    if m == 0:
                        pe.wait_ge(relu_done, b * NFC + NFT)
                        for s in stacked:
                            pe.wait_ge(s, (b + 1) * 2 * STACK_DMAS * 16)
                    else:
                        pe.wait_ge(max_done, b * NMAX + m)
                    for g in range(qt * P // G + 1):
                        w = min(G, (qt + 1) * P - g * G)
                        ins = pe.matmul(flat[:, g * G:g * G + w], q_stack[rows, h // 2, qt * P:(qt + 1) * P],
                                        k_stack[rows, h // 2, g * G:g * G + w], start=True, stop=True)
                    ins.then_inc(max_ps, 1)
                pe.wait_ge(max_done, (b + 1) * NMAX)
                for qt in range(NT):
                    ins = pe.transpose(pair[3][0:H, qt // 4, (qt % 4) * P:(qt % 4 + 1) * P], row_max[:, qt, :], ident)
                ins.then_inc(max_ps, 1)

            def mlp(b, last):
                def expand(i):
                    g, f = i // NFT, i % NFT
                    cols, m = slice(g * G, (g + 1) * G), slice(f * P, (f + 1) * P)
                    if i < 4:
                        if last is not None and i % 2 == 0:
                            pe.wait_ge(out_done, last * 4 + i + 2)
                    else:
                        pe.wait_ge(relu_done, b * NFC + i - 3)
                    if i == NFT + 1:
                        pe.wait_ge(flag_done, b + 1)
                    parts = [p for k in range(KD) for p in (
                        (wfc_hi[:, k, m], xT_hi[:, k, cols]), (wfc_lo[:, k, m], xT_hi[:, k, cols]),
                        (wfc_hi[:, k, m], xT_lo[:, k, cols]))]
                    split_product(pair[i // 2 % 2][:, i % 2, :], parts).then_inc(fc_ps, 1)

                def contract(i):
                    g, f = i // NFT, i % NFT
                    if i == 0:
                        pe.wait_ge(norm_used, b * 3 + 3)
                    pe.wait_ge(h_lo_done, b * NFC + i + 1)
                    for t in range(4):
                        cols = slice(t * P, (t + 1) * P)
                        bank = pair[2 + g][:, t // 2, (t % 2) * D:(t % 2 + 1) * D]
                        for n, (h, w) in enumerate(((h_hi, wproj_hi), (h_hi, wproj_lo), (h_lo, wproj_hi))):
                            ins = pe.matmul(bank, h[i % 3][:, cols], w[:, f, :], start=f == 0 and n == 0 and t % 2 == 0,
                                            stop=f == NFT - 1 and n == 2, skip_group_check=True)
                    ins.then_inc(proj_done, 1)

                for i in range(NFC + 2):
                    if i < NFC:
                        expand(i)
                    if i >= 2:
                        contract(i - 2)
                    if i == NFT + 1:
                        loose = pe.value_load(flag[0:1, 0:1], min_val=0, max_val=1)
                        with pe.If(loose > 0):
                            row_maxima(b)
                        with pe.Else():
                            pe.sem_inc(max_ps, NMAX + 1)

            def attention(b):
                def scores(n):
                    quad, (kt, g) = n // NU, UNITS[n % NU]
                    q0 = first_query(kt, g)
                    for pr in range(2):
                        m = 2 * n + pr
                        if m >= NSLOT:
                            pe.wait_ge(exp_done, b * 2 * NUNIT + m - NSLOT + 1)
                        elif m == 2:
                            pe.wait_ge(resid_done, b * NG + 1)
                        for half in range(2):
                            rows = slice(64 * half, 64 * half + 64)
                            tile = 2 * quad + pr
                            ins = pe.matmul(pair[m % NSLOT][:, half, 0:(g + 1) * G - q0],
                                            k_stack[rows, tile, kt * P:(kt + 1) * P], q_stack[rows, tile, q0:(g + 1) * G],
                                            start=True, stop=True)
                        ins.then_inc(scores_ps, 1)

                def weigh(n):
                    quad, (kt, g) = n // NU, UNITS[n % NU]
                    q0 = first_query(kt, g)
                    pe.wait_ge(exp_done, b * 2 * NUNIT + 2 * n + 2)
                    if DIAG[n % NU]:
                        pe.wait_ge(mask_done, b * NQUAD * ND + diag_before(n) + 1)
                    if kt == 0:
                        if quad:
                            pe.wait_ge(numer_done, (b * NQUAD + quad - 1) * 2 + g + 1)
                        else:
                            pe.wait_ge(resid_done, b * NG + NG)
                    last = kt == max(k for k, gg in UNITS if gg == g)
                    for i in range(4):
                        ins = pe.matmul(pair[OPAIR][32 * i:32 * i + VW, g, q0 - g * G:G], v_sb[:, kt, 4 * quad + i, :],
                                        probs[n % NPB][:, i, 0:(g + 1) * G - q0], start=kt == 0, stop=last)
                    ins.then_inc(pv_done, 1)

                for s in stacked:
                    pe.wait_ge(s, (b + 1) * 2 * STACK_DMAS * 16)
                pe.wait_ge(shift_in, (b + 1) * 4 * 16)
                for n in range(NUNIT + LAG):
                    if n < NUNIT:
                        scores(n)
                    if n >= LAG:
                        weigh(n - LAG)

            pe.wait_ge(w_split, 9)
            pe.wait_ge(consts_in, 16 * 6)
            pe.wait_ge(cleared, 3)
            transposes(0)
            queries_keys(0, None)
            values(0)
            norms(0)
            mlp(0, None)
            with pe.Fori(0, B - 1) as b:
                attention(b)
                transposes(b + 1)
                queries_keys(b + 1, b)
                values(b + 1)
                output(b, b + 1)
                norms(b + 1)
                mlp(b + 1, b)
            attention(B - 1)
            output(B - 1, None)


def rotary_tables():
    inv_freq = (np.float32(1.0) / np.float32(THETA) ** (np.arange(0, DK, 2, dtype=np.float32) / np.float32(DK))).astype(np.float32)
    angles = np.arange(S, dtype=np.float32)[None, :] * inv_freq[:, None]
    rows = np.tile(np.repeat(np.arange(NF), NTILE), 2)
    return np.stack([np.cos(angles), np.sin(angles)]).astype(np.float32)[:, rows, :]


def fixed_masks():
    i = np.arange(P)
    ident = (i[:, None] == i[None, :]).astype(np.float32)
    causal = np.where(i[None, :] <= i[:, None], 0.0, MASKED).astype(np.float32)
    head = i // 64 * NTILE + i % NTILE
    mine = (head[:, None] == np.arange(H)[None, :]).astype(np.float32)
    return np.concatenate([ident, causal, mine, np.float32(BOUND_HALF) * mine, -mine], axis=1)


def kernel(**inputs):
    import concourse.bacc as _bacc
    from concourse.bass_utils import run_bass_kernel_spmd as _run

    a = {n.split("_", 1)[1]: np.ascontiguousarray(inputs[n]) for n in inputs}
    half, freq, tile = (v.ravel() for v in np.meshgrid(np.arange(2), np.arange(NF), np.arange(NTILE), indexing="ij"))
    column = (2 * tile + half) * DK + 2 * freq
    order = [column, column + 1]
    laid = {
        "x": a["attn_x"],
        "wqk": np.concatenate([a[w][o].T for w in ("attn_Wq", "attn_Wk") for o in order], axis=1),
        "bqk": np.stack([a[v][o] for v in ("attn_bq", "attn_bk") for o in order], axis=1),
        "wv": a["attn_Wv"].T,
        "bv": a["attn_bv"],
        "wfc": a["ffn_W_fc"].T,
        "wproj": a["ffn_W_proj"].T,
        "wo": a["attn_Wo"].T,
        "bo": a["attn_bo"],
        "tables": rotary_tables(),
        "consts": fixed_masks(),
    }
    nc = _bacc.Bacc("TRN2", target_bir_lowering=False, num_devices=1, dynamic_dma_scratch_size=1024)
    arrays, args = {}, []
    for name, v in laid.items():
        v = np.ascontiguousarray(v)
        arrays[f"in_{name}"] = v
        args.append(nc.dram_tensor(f"in_{name}", v.shape, mybir.dt.from_np(v.dtype), kind="ExternalInput").ap())
    args.append(nc.dram_tensor("out", (B, S, D), F32, kind="ExternalOutput").ap())
    layer_kernel(nc, *args)
    r = _run(nc, [arrays], core_ids=[0])
    return r.results[0]["out"]
```

```python
from contextlib import ExitStack

import numpy as np
import concourse.bass as bass
from concourse import mybir

F32, F32R, BF16, I32 = mybir.dt.float32, mybir.dt.float32r, mybir.dt.bfloat16, mybir.dt.int32
ALU, ACT, AX = mybir.AluOpType, mybir.ActivationFunctionType, mybir.AxisListType

P = 128
B, S, D = 16, 1024, 256
H, DK, F = 16, 16, 1024
NF = DK // 2
THETA, LN_EPS, SCALE = 10000.0, 1e-5, 1.0 / DK ** 0.5
BETA, THRESHOLD, STEPS = 0.9, 1.0, 5
NT = S // P
G = 512
NG = S // G
KD = D // P
NFT = F // P
NTILE = H // 2
NQUAD = H // 4
VW = DK + 1
BOUND_HALF = 131 / 256
GAP_LIMIT = 64.0 / SCALE
MASKED = -1e30

UNITS = [(0, 0), (3, 0), (2, 0), (1, 0), (0, 1), (7, 1), (6, 1), (5, 1), (4, 1), (1, 1), (2, 1), (3, 1)]
assert sorted(UNITS) == [(kt, g) for kt in range(NT) for g in range(NG) if (g + 1) * G > kt * P]
NU = len(UNITS)
NUNIT = NQUAD * NU
GROUP_END = [n for n in range(NU) if n + 1 == NU or UNITS[n + 1][1] != UNITS[n][1]]
DIAG = [kt // (G // P) == g for kt, g in UNITS]
ND = sum(DIAG)
LAG = 2
NPB = 3
NSLOT = 2


def first_query(kt, g):
    return max(kt * P, g * G)


def width(n):
    kt, g = UNITS[n % NU]
    return (g + 1) * G - first_query(kt, g)


def diag_before(n):
    return n // NU * ND + sum(DIAG[:n % NU])


NFC = NG * NFT
FRONT = 4
MLP_END = NUNIT - 4


def mlp_halves():
    items = [item for i in range(FRONT, NFC) for item in ((0, i), (1, i - 1))] + [(1, NFC - 1)]
    halves = [(c, i, half) for c, i in items for half in range(2)]
    total, done, steps, taken = sum(width(n) for n in range(MLP_END)), 0, [], 0
    for n in range(NUNIT + LAG):
        done += width(n) if n < MLP_END else 0
        upto = len(halves) * done // total
        steps.append(halves[taken:upto])
        taken = upto
    return steps


def spike_thresholds():
    f = np.float32

    def count(y):
        mem, spikes = f(0), 0
        for _ in range(STEPS):
            reset = f(mem - f(THRESHOLD) > 0)
            mem = f(f(f(BETA) * mem + y) - reset * f(THRESHOLD))
            spikes += bool(mem - f(THRESHOLD) > 0)
        return spikes

    edges = []
    for n in range(1, STEPS + 1):
        lo, hi = f(0), f(2)
        while np.nextafter(lo, hi) < hi:
            mid = f((lo + hi) / f(2))
            mid = mid if lo < mid < hi else np.nextafter(lo, hi)
            lo, hi = (lo, mid) if count(mid) >= n else (mid, hi)
        edges.append(float(lo))
    return edges


def layer_kernel(nc, x, wqk, bqk, wv, bv, wfc, wproj, wo, bo, tables, consts, out):
    edges = spike_thresholds()
    with ExitStack() as ctx:
        KB = 1024
        arena_at = (nc.sbuf_base + 31) // 32 * 32
        ctx.enter_context(nc.sbuf_tensor("arena", [P, 32 * KB // 4], F32))

        def shared(name, shape, dt, at):
            return nc.alloc_sbuf_tensor_at(name, shape, dt, offset=arena_at + at)

        def sb(name, shape, dt=F32):
            return ctx.enter_context(nc.sbuf_tensor(name, shape, dt))

        probs = [shared(f"probs{i}", [P, 4, G], F32, 8 * KB * i) for i in range(NPB)]
        planes = [shared(f"planes{i}", [P, 2, 2, G], F32R, 8 * KB * i) for i in range(2)]
        rot = [shared(f"rot{i}", [P, 2, G], F32, (16 + 4 * i) * KB) for i in range(2)]
        rot_b = [shared(f"rot_b{i}", [P, 2, G], F32, (24 + 4 * i) * KB) for i in range(2)]
        wqk_in = shared("wqk_in", [P, KD, 4 * P], F32, 0)
        wv_in = shared("wv_in", [P, KD, D], F32, 4 * KB)
        wfc_in = shared("wfc_in", [P, KD, F], F32, 8 * KB)
        wproj_in = shared("wproj_in", [P, NFT, D], F32, 16 * KB)

        xn_at = (nc.sbuf_base + 31) // 32 * 32
        xn = sb("xn", [P, NT, D])
        squares = nc.alloc_sbuf_tensor_at("squares", [P, 4, 2, G], BF16, offset=xn_at)

        h_sq = sb("h_sq", [P, G])
        h_hi, h_lo = ([sb(f"{n}{i}", [P, G], F32R) for i in range(2)] for n in ("h_hi", "h_lo"))
        count = sb("count", [P, G], BF16)
        q_stack = sb("q_stack", [P, NTILE, S], F32R)
        k_stack = sb("k_stack", [P, NTILE, S], F32R)
        wqk_hi, wqk_lo = sb("wqk_hi", [P, KD, 4 * P], F32R), sb("wqk_lo", [P, KD, 4 * P], F32R)
        wv_hi, wv_lo = sb("wv_hi", [P, KD, D], F32R), sb("wv_lo", [P, KD, D], F32R)
        wfc_hi, wfc_lo = sb("wfc_hi", [P, KD, F], F32R), sb("wfc_lo", [P, KD, F], F32R)
        wproj_hi, wproj_lo = sb("wproj_hi", [P, NFT, D], F32R), sb("wproj_lo", [P, NFT, D], F32R)
        wo_sb = sb("wo_sb", [P, KD, D])
        table = sb("table", [P, 2, S])
        xT_hi, xT_lo = sb("xT_hi", [P, KD, S], F32R), sb("xT_lo", [P, KD, S], F32R)
        v_sb = sb("v_sb", [P, NT, H, VW])
        resid = sb("resid", [P, NT, D])
        attn = sb("attn", [P, KD, S])
        numer_at = (nc.sbuf_base + 31) // 32 * 32
        numer = sb("numer", [P, S])
        shift = nc.alloc_sbuf_tensor_at("shift", [H, S], F32R, offset=numer_at)
        own_qk = nc.alloc_sbuf_tensor_at("own_qk", [P, NG, 2, G], BF16, offset=numer_at)
        denom = sb("denom", [64, P])
        recip_at = (nc.sbuf_base + 31) // 32 * 32
        recip_rows = sb("recip_rows", [P, S])
        y_sb = nc.alloc_sbuf_tensor_at("y_sb", [P, 2, G], F32, offset=recip_at)
        out_sb = [nc.alloc_sbuf_tensor_at(f"out_sb{i}", [P, 2, D], F32, offset=recip_at + 2 * KB * i) for i in range(2)]
        const = sb("const", [P, 2 * P + 3 * H])
        ident, causal = const[:, 0:P], const[:, P:2 * P]
        sel = sb("sel", [P, 3, H], BF16)
        bqk_sb, neg_bqk = sb("bqk_sb", [P, 4]), sb("neg_bqk", [P, 4])
        bv_sb, bo_sb = sb("bv_sb", [P, D]), sb("bo_sb", [P, D])
        stats = sb("stats", [P, NT, 6])
        mean, var, mean_gap, rstd = (sb(n, [P, NT]) for n in ("mean", "var", "mean_gap", "rstd"))
        ln_a, ln_b, neg_half = (sb(n, [P, NT]) for n in ("ln_a", "ln_b", "neg_half"))
        k_max, q_gap, gap, gap_all = (sb(n, [H, 1]) for n in ("k_max", "q_gap", "gap", "gap_all"))
        flag = sb("flag", [1, 1], I32)
        row_max = sb("row_max", [P, NT, H])

        recip_dram = nc.dram_tensor("recip_dram", [KD, H // KD, S], F32, kind="Internal").ap()

        pair = [ctx.enter_context(nc.psum_tensor(f"pair{i}", [P, 2, G], F32)) for i in range(4)]
        pv_bank, fc_bank, proj_bank = pair[2][:, 0, :], pair[2][:, 1, :], pair[3]
        xT_bank = (pair[2][:, 1, :], pair[0][:, 0, :], pair[0][:, 1, :], pair[2][:, 1, :])
        QK_PAIR = (1, 3, 0, 1)
        v_bank = (pair[3][:, 0, :], pair[3][:, 1, :], pair[2][:, 0, :], pair[2][:, 1, :])

        def sem(name):
            return ctx.enter_context(nc.semaphore(name))

        w_in, w_split, consts_in, cleared = sem("w_in"), sem("w_split"), sem("consts_in"), sem("cleared")
        x_in, resid_in = sem("x_in"), sem("resid_in")
        stats_done, var_done = sem("stats_done"), sem("var_done")
        ln_step, vec_step = sem("ln_step"), sem("vec_step")
        rstd_done, xn_done, xb_done = sem("rstd_done"), sem("xn_done"), sem("xb_done")
        xT_ps, xT_hi_done, xT_lo_done = sem("xT_ps"), sem("xT_hi_done"), sem("xT_lo_done")
        qk_ps, rot_done, rot_sum = sem("qk_ps"), sem("rot_done"), sem("rot_sum")
        plane_hi, plane_lo, sq_done = sem("plane_hi"), sem("plane_lo"), sem("sq_done")
        stacked = [sem("stacked0"), sem("stacked1")]
        v_ps, v_copied, v_done = sem("v_ps"), sem("v_copied"), sem("v_done")
        wo_ps, out_done = sem("wo_ps"), sem("out_done")
        out_sent = [sem("out_sent0"), sem("out_sent1")]
        own_done, norm_ps, norm_used, gap_done, gap_max, flag_done = (
            sem(n) for n in ("own_done", "norm_ps", "norm_used", "gap_done", "gap_max", "flag_done"))
        max_ps, max_done, max_step = sem("max_ps"), sem("max_done"), sem("max_step")
        shift_done, shift_in = sem("shift_done"), sem("shift_in")
        fc_ps, relu_done, sq_h, h_hi_done, h_lo_done, proj_done = (
            sem(n) for n in ("fc_ps", "relu_done", "sq_h", "h_hi_done", "h_lo_done", "proj_done"))
        y_copied, spike_step, resid_done = sem("y_copied"), sem("spike_step"), sem("resid_done")
        scores_ps, exp_done, mask_done, pv_done = (
            sem(n) for n in ("scores_ps", "exp_done", "mask_done", "pv_done"))
        numer_done = sem("numer_done")
        numer_in = [sem("numer_in0"), sem("numer_in1")]
        denom_in, recip_done = sem("denom_in"), sem("recip_done")
        recip_out, recip_in, attn_done = sem("recip_out"), sem("recip_in"), sem("attn_done")
        NMAX = H * NT
        STACK_DMAS = 3 * 2

        HALVES = mlp_halves()
        STEPS_ALL = range(NUNIT + LAG)
        CONTRACTED = {i: n for n in STEPS_ALL for c, i, half in HALVES[n] if c and half}
        XT_AT = {NUNIT - 1: 0, NUNIT: 1}
        Y_AT = {CONTRACTED[g * NFT + NFT - 1]: g for g in range(NG)}
        SPIKES_AT = {CONTRACTED[g * NFT + NFT - 1] + 2 * a + part: (g, a, range(3 * part, 3 * part + 3))
                     for g in range(NG) for a in range(2) for part in range(2)}
        assert max(SPIKES_AT) < NUNIT + LAG
        GROUP_ENDS = {q * NU + n + LAG: (q, g) for q in range(NQUAD) for g, n in enumerate(GROUP_END)}
        STATS_AT, ROOT_AT, XN_AT, BO_AT = 4, 14, 18, 3
        INVERT_AT, DIVIDE_AT = 2 * NU + LAG + 3, 2 * NU + LAG + 9

        stood = sem("stood")

        def alone(eng, s, value):
            eng.wait_ge(s, value)
            eng.sem_inc(stood, 1)

        block = ctx.enter_context(nc.Block())

        @block.sync
        def _(sp):
            for dst, src in ((wqk_in, wqk), (wv_in, wv), (wfc_in, wfc), (wproj_in, wproj)):
                sp.dma_start(dst[:, :, :], src.rearrange("(k p) n -> p k n", p=P)).then_inc(w_in, 16)
            sp.dma_start(const[:, :], consts).then_inc(consts_in, 16)
            sp.dma_start(wo_sb[:, :, :], wo.rearrange("(k p) n -> p k n", p=P)).then_inc(consts_in, 16)
            sp.dma_start(table[:, :, :], tables.rearrange("t p s -> p t s")).then_inc(consts_in, 16)
            sp.dma_start(bqk_sb[:, :], bqk).then_inc(consts_in, 16)
            sp.dma_start(bv_sb[:, :], bv.partition_broadcast(P)).then_inc(consts_in, 16)
            sp.dma_start(bo_sb[:, :], bo.partition_broadcast(P)).then_inc(consts_in, 16)

            def load_x(b, last):
                if last is not None:
                    alone(sp, norm_ps, last + 1)
                sp.dma_start(xn[:, :, :], x[b].rearrange("(t p) d -> p t d", p=P)).then_inc(x_in, 16)

            def load_resid(b):
                sp.dma_start(resid[:, :, :], x[b].rearrange("(t p) d -> p t d", p=P)).then_inc(resid_in, 16)

            def stack(b):
                for u in range(4):
                    g, is_k = u // 2, u % 2
                    dst = k_stack if is_k else q_stack
                    buf = planes[u % 2]
                    for lo in range(2):
                        sp.wait_ge(plane_lo if lo else plane_hi, b * 4 + u + 1)
                        for part in range(3):
                            if lo != (part == (1 if is_k else 2)):
                                continue
                            for eo in range(2):
                                sp.dma_start(dst[2 * part + eo:P:NF, :, g * G:(g + 1) * G].bitcast(F32),
                                             buf[:, lo, eo, :].bitcast(F32)).then_inc(stacked[u % 2], 16)

            def store(b):
                for n in range(4):
                    alone(sp, out_done, b * 4 + n + 1)
                    sp.dma_start(out[b].rearrange("(t p) d -> p t d", p=P)[:, 2 * n:2 * n + 2, :],
                                 out_sb[n % 2][:, :, :]).then_inc(out_sent[n % 2], 16)

            def stored(b):
                for s in out_sent:
                    alone(sp, s, (b + 1) * 2 * 16)

            def load_shift(b):
                for n in range(2):
                    if n == 0:
                        sp.wait_ge(norm_used, b * 3 + 3)
                    else:
                        alone(sp, shift_in, b * 2 * 16 + 16)
                        sp.wait_ge(shift_done, b + 1)
                    sp.dma_start(q_stack[6:P:64, :, :].bitcast(F32), shift[:, :].bitcast(F32)).then_inc(shift_in, 16)

            def gather(b):
                for quad in range(NQUAD):
                    k, base = quad // 2, quad % 2 * 64
                    sp.wait_ge(numer_done, (b * NQUAD + quad) * 2 + 2)
                    sp.dma_start(denom[base // 2:base // 2 + 32, :], numer[DK:P:32, :]).then_inc(denom_in, 16)
                    for i in range(4):
                        sp.dma_start(attn[base + DK * i:base + DK * (i + 1), k, :],
                                     numer[32 * i:32 * i + DK, :]).then_inc(numer_in[k], 16)
                    if quad % 2:
                        sp.wait_ge(recip_done, b * KD + k + 1)
                        sp.dma_start(recip_dram[k].rearrange("h (c q) -> (h c) q", q=P), denom[:, :]
                                     ).then_inc(recip_out, 16)
                        alone(sp, recip_out, (b * KD + k + 1) * 16)
                        sp.dma_start(recip_rows[:, :],
                                     recip_dram[k].unsqueeze(1).broadcast_to([H // KD, DK, S])
                                     ).then_inc(recip_in, 16)

            load_x(0, None)
            load_resid(0)
            stack(0)
            load_shift(0)
            with sp.Fori(0, B - 1) as b:
                load_x(b + 1, b)
                gather(b)
                stack(b + 1)
                store(b)
                load_resid(b + 1)
                stored(b)
                load_shift(b + 1)
            gather(B - 1)
            store(B - 1)
            stored(B - 1)

        @block.gpsimd
        def _(pool):
            def chained(ins):
                ins.then_inc(ln_step, 1)

            pool.memset(v_sb[:, :, :, DK:VW], 1.0).then_inc(cleared, 1)
            pool.memset(neg_half[:, :], -0.5).then_inc(ln_step, 1)
            pool.memset(q_stack[:, :, :].bitcast(F32), 0.0).then_inc(cleared, 1)
            pool.wait_ge(ln_step, 1)
            LN_OPS = 5

            def root(b):
                base = b * LN_OPS + 1
                pool.wait_ge(var_done, b + 1)
                chained(pool.tensor_tensor(ln_a[:, :], var[:, :], neg_half[:, :], ALU.pow))
                pool.wait_ge(ln_step, base + 1)
                chained(pool.tensor_tensor(ln_b[:, :], ln_a[:, :], ln_a[:, :], ALU.mult))
                pool.wait_ge(ln_step, base + 2)
                chained(pool.tensor_tensor(ln_b[:, :], ln_b[:, :], var[:, :], ALU.mult))
                alone(pool, ln_step, base + 3)
                chained(pool.tensor_scalar(ln_b[:, :], ln_b[:, :], -0.5, 1.5, ALU.mult, ALU.add))
                pool.wait_ge(ln_step, base + 4)
                chained(pool.tensor_tensor(ln_b[:, :], ln_b[:, :], ln_a[:, :], ALU.mult))
                alone(pool, ln_step, base + 5)
                pool.tensor_copy(rstd[:, :], ln_b[:, :]).then_inc(rstd_done, 1)

            def add_bo(b, t):
                if t == 0:
                    pool.wait_ge(resid_in, b * 16 + 16)
                pool.tensor_tensor(resid[:, t, :], resid[:, t, :], bo_sb[:, :], ALU.add).then_inc(xb_done, 1)

            def add_bv(b, tiles):
                for t in tiles:
                    if t % 2 == 0:
                        pool.wait_ge(v_copied, b * 4 + t // 2 + 1)
                    heads = v_sb[:, t, :, 0:DK]
                    pool.tensor_tensor(heads, heads, bv_sb[:, :].rearrange("p (h d) -> p h d", d=DK), ALU.add
                                       ).then_inc(v_done, 1)

            def rotary(b, last):
                for u in range(4):
                    pool.wait_ge(rot_done, b * 4 + u + 1)
                    pool.tensor_tensor(rot[u % 2][:, :, :], rot[u % 2][:, :, :], rot_b[u % 2][:, :, :], ALU.add
                                       ).then_inc(rot_sum, 1)
                    if u % 2:
                        if u == 1 and last is not None:
                            pool.wait_ge(numer_in[1], (last + 1) * 2 * 4 * 16)
                            pool.wait_ge(denom_in, (last + 1) * NQUAD * 16)
                        pool.wait_ge(plane_hi, b * 4 + u + 1)
                        q, k = (planes[i][:, 0, :, :].bitcast(F32) for i in range(2))
                        pool.tensor_tensor(own_qk[:, u // 2, :, :], q, k, ALU.mult).then_inc(own_done, 1)

            def widest_gap(b):
                alone(pool, gap_done, b + 1)
                pool.partition_all_reduce(gap_all[:, :], gap[:, :], H, bass.bass_isa.ReduceOp.max
                                          ).then_inc(gap_max, 1)

            def h_low(b, i):
                if i >= 2:
                    pool.wait_ge(proj_done, b * NFC + i - 1)
                pool.wait_ge(h_hi_done, b * NFC + i + 1)
                pool.tensor_tensor(h_lo[i % 2][:, :], h_sq[:, :], h_hi[i % 2][:, :].bitcast(F32),
                                   ALU.subtract).then_inc(h_lo_done, 1)

            def mask(b, n):
                alone(pool, exp_done, (b * NUNIT + n) * 2 + 2)
                view = probs[n % NPB][:, :, 0:P]
                pool.affine_select(view, view, [[0, 4], [1, P]], ALU.is_ge, 0.0, base=0,
                                   channel_multiplier=-1).then_inc(mask_done, 1)

            def projection(b, last):
                rotary(b, last)
                add_bv(b, range(4))
                h_low(b, 0)
                widest_gap(b)
                add_bv(b, range(4, NT))
                for i in range(1, FRONT):
                    h_low(b, i)

            def attention(b, more):
                for n in STEPS_ALL:
                    for c, i, half in HALVES[n]:
                        if not c and half:
                            h_low(b, i)
                    if n < NUNIT and DIAG[n % NU]:
                        mask(b, n)
                    if BO_AT <= n < BO_AT + NT:
                        add_bo(b, n - BO_AT)
                    if n == ROOT_AT and more:
                        root(b + 1)

            pool.wait_ge(consts_in, 16 * 6)
            root(0)
            projection(0, None)
            with pool.Fori(0, B - 1) as b:
                attention(b, True)
                projection(b + 1, b)
            attention(B - 1, False)

        @block.scalar
        def _(act):
            def high_xT(b, n):
                g, k = n // 2, n % 2
                act.wait_ge(xT_ps, b * 4 + n + 1)
                act.activation(xT_hi[:, k, g * G:(g + 1) * G], xT_bank[n], ACT.Copy).then_inc(xT_hi_done, 1)

            def high_qk(b, u):
                act.wait_ge(rot_sum, b * 4 + u + 1)
                if u >= 2:
                    act.wait_ge(stacked[u % 2], (b * 2 + 1) * STACK_DMAS * 16)
                    act.wait_ge(own_done, b * NG + 1)
                act.activation(planes[u % 2][:, 0, :, :], rot[u % 2][:, :, :], ACT.Copy).then_inc(plane_hi, 1)
                act.activation(squares[:, u, :, :], rot[u % 2][:, :, :], ACT.Square).then_inc(sq_done, 1)

            def take_v(b, n):
                act.wait_ge(v_ps, b * 4 + n + 1)
                act.activation(v_sb[:, 2 * n:2 * n + 2, :, 0:DK], v_bank[n].rearrange(
                    "p (t h d) -> p t h d", t=2, d=DK), ACT.Copy).then_inc(v_copied, 1)

            def rectify(b, i):
                if i >= 1:
                    act.wait_ge(h_lo_done, b * NFC + i)
                act.wait_ge(fc_ps, b * NFC + i + 1)
                act.activation(h_sq[:, :], fc_bank, ACT.Relu).then_inc(relu_done, 1)

            def projection(b):
                high_xT(b, 2)
                high_xT(b, 3)
                high_qk(b, 0)
                high_qk(b, 1)
                for n in range(4):
                    take_v(b, n)
                high_qk(b, 2)
                rectify(b, 0)
                high_qk(b, 3)
                for i in range(1, FRONT):
                    rectify(b, i)

            def attention(b, more):
                for n in STEPS_ALL:
                    if n < NUNIT:
                        w = width(n)
                        if n >= NPB:
                            act.wait_ge(pv_done, b * NUNIT + n - NPB + 1)
                        for pr in range(2):
                            m = 2 * n + pr
                            act.wait_ge(scores_ps, b * 2 * NUNIT + m + 1)
                            act.activation(probs[n % NPB][:, 2 * pr:2 * pr + 2, 0:w], pair[m % NSLOT][:, :, 0:w],
                                           ACT.Exp, scale=SCALE).then_inc(exp_done, 1)
                    for c, i, half in HALVES[n]:
                        if not c and half:
                            rectify(b, i)
                    if more and n in XT_AT:
                        high_xT(b + 1, XT_AT[n])

            act.wait_ge(w_split, 9)
            for n in range(2):
                high_xT(0, n)
            projection(0)
            with act.Fori(0, B - 1) as b:
                attention(b, True)
                projection(b + 1)
            attention(B - 1, False)

        @block.vector
        def _(dve):
            dve.memset(k_stack[:, :, :].bitcast(F32), 1.0).then_inc(cleared, 1)
            dve.wait_ge(w_in, 16 * 4)
            for hi, lo, whole in ((wqk_hi, wqk_lo, wqk_in), (wv_hi, wv_lo, wv_in), (wfc_hi, wfc_lo, wfc_in),
                                  (wproj_hi, wproj_lo, wproj_in)):
                dve.tensor_copy(hi[:, :, :], whole[:, :, :]).then_inc(w_split, 1)
            for n, (hi, lo, whole) in enumerate(((wqk_hi, wqk_lo, wqk_in), (wv_hi, wv_lo, wv_in),
                                                 (wfc_hi, wfc_lo, wfc_in), (wproj_hi, wproj_lo, wproj_in))):
                dve.wait_ge(w_split, 4 + n)
                dve.tensor_tensor(lo[:, :, :], whole[:, :, :], hi[:, :, :].bitcast(F32), ALU.subtract
                                  ).then_inc(w_split, 1)
            dve.wait_ge(consts_in, 16 * 6)
            dve.tensor_copy(sel[:, :, :].rearrange("p a h -> p (a h)"), const[:, 2 * P:2 * P + 3 * H]).then_inc(vec_step, 1)
            dve.tensor_scalar(neg_bqk[:, :], bqk_sb[:, :], -1.0, None, ALU.mult).then_inc(w_split, 1)
            dve.wait_ge(w_split, 9)

            def statistics(b, t):
                if t == 0:
                    dve.wait_ge(x_in, b * 16 + 16)
                dve.bn_stats(stats[:, t, :], xn[:, t, :]).then_inc(stats_done, 1)

            def variance(b):
                base = b * 6 + 1
                dve.wait_ge(stats_done, b * NT + NT)
                dve.tensor_tensor(mean_gap[:, :], stats[:, :, 1], stats[:, :, 4], ALU.subtract).then_inc(vec_step, 1)
                dve.tensor_tensor(mean[:, :], stats[:, :, 1], stats[:, :, 4], ALU.add).then_inc(vec_step, 1)
                dve.tensor_tensor(var[:, :], stats[:, :, 2], stats[:, :, 5], ALU.add).then_inc(vec_step, 1)
                dve.wait_ge(vec_step, base + 3)
                dve.tensor_tensor(mean_gap[:, :], mean_gap[:, :], mean_gap[:, :], ALU.mult).then_inc(vec_step, 1)
                dve.tensor_scalar(mean[:, :], mean[:, :], 0.5, None, ALU.mult).then_inc(vec_step, 1)
                dve.tensor_scalar(var[:, :], var[:, :], 1.0 / D, LN_EPS, ALU.mult, ALU.add).then_inc(vec_step, 1)
                dve.wait_ge(vec_step, base + 6)
                dve.scalar_tensor_tensor(var[:, :], mean_gap[:, :], 0.25, var[:, :], ALU.mult, ALU.add
                                         ).then_inc(var_done, 1)

            def normalise(b, t):
                dve.wait_ge(rstd_done, b + 1)
                dve.tensor_scalar(xn[:, t, :], xn[:, t, :], mean[:, t:t + 1], rstd[:, t:t + 1],
                                  ALU.subtract, ALU.mult).then_inc(xn_done, 1)

            def low_xT(b, n):
                g, k = n // 2, n % 2
                cols = slice(g * G, (g + 1) * G)
                dve.wait_ge(xT_hi_done, b * 4 + n + 1)
                dve.tensor_tensor(xT_lo[:, k, cols], xT_bank[n], xT_hi[:, k, cols].bitcast(F32),
                                  ALU.subtract).then_inc(xT_lo_done, 1)

            def rotate(b, u):
                g, is_k = u // 2, u % 2
                cos, sin = (table[:, n, g * G:(g + 1) * G] for n in range(2))
                even, odd = (pair[QK_PAIR[u]][:, eo, :] for eo in range(2))
                e_bias, o_bias = (bqk_sb[:, 2 * is_k + eo:2 * is_k + eo + 1] for eo in range(2))
                neg_o_bias = neg_bqk[:, 2 * is_k + 1:2 * is_k + 2]
                dve.wait_ge(qk_ps, b * 4 + u + 1)
                if u >= 2:
                    dve.wait_ge(rot_sum, b * 4 + u - 1)
                    dve.wait_ge(sq_done, b * 4 + u - 1)
                    dve.wait_ge(plane_lo, b * 4 + u - 1)
                part = rot[u % 2]
                dve.scalar_tensor_tensor(part[:, 0, :], even, e_bias, cos, ALU.add, ALU.mult)
                dve.scalar_tensor_tensor(part[:, 1, :], even, e_bias, sin, ALU.add, ALU.mult)
                dve.scalar_tensor_tensor(rot_b[u % 2][:, 0, :], odd, neg_o_bias, sin, ALU.subtract, ALU.mult, reverse0=True)
                dve.scalar_tensor_tensor(rot_b[u % 2][:, 1, :], odd, o_bias, cos, ALU.add, ALU.mult).then_inc(rot_done, 1)

            def low_qk(b, u):
                dve.wait_ge(plane_hi, b * 4 + u + 1)
                dve.tensor_tensor(planes[u % 2][:, 1, :, :], rot[u % 2][:, :, :],
                                  planes[u % 2][:, 0, :, :].bitcast(F32), ALU.subtract).then_inc(plane_lo, 1)

            def invert(b, k):
                dve.wait_ge(denom_in, (b * NQUAD + 2 * k + 2) * 16)
                dve.reciprocal(denom[:, :], denom[:, :]).then_inc(recip_done, 1)

            def divide(b, k):
                dve.wait_ge(numer_in[k], (b + 1) * 2 * 4 * 16)
                dve.wait_ge(recip_in, (b * KD + k + 1) * 16)
                dve.tensor_tensor(attn[:, k, :], attn[:, k, :], recip_rows[:, :], ALU.mult).then_inc(attn_done, 1)

            def finish(b, banks):
                for n in banks:
                    if n >= 2:
                        dve.wait_ge(out_sent[n % 2], (b * 2 + 1) * 16)
                    dve.wait_ge(wo_ps, b * 4 + n + 1)
                    dve.tensor_tensor(out_sb[n % 2][:, :, :], pair[n // 2][:, n % 2, :].rearrange(
                        "p (t d) -> p t d", d=D), resid[:, 2 * n:2 * n + 2, :], ALU.add).then_inc(out_done, 1)

            def bound(b):
                dve.wait_ge(norm_ps, b + 1)
                dve.tensor_reduce(k_max[:, :], pair[3][64:64 + H, :, :], AX.XY, ALU.max).then_inc(norm_used, 1)
                dve.tensor_reduce(q_gap[:, :], pair[3][32:32 + H, :, :], AX.XY, ALU.max).then_inc(norm_used, 1)
                dve.wait_ge(norm_used, b * 3 + 2)
                dve.scalar_tensor_tensor(gap[:, :], k_max[:, :], BOUND_HALF, q_gap[:, :], ALU.mult, ALU.add
                                         ).then_inc(gap_done, 1)
                dve.tensor_scalar(shift[0:H, :].rearrange("h (g q) -> h g q", q=G), pair[3][0:H, :, :],
                                  k_max[:, 0:1], -BOUND_HALF, ALU.add, ALU.mult).then_inc(norm_used, 1)

            def raise_flag(b):
                dve.wait_ge(gap_max, b + 1)
                dve.tensor_scalar(flag[:, :], gap_all[0:1, :], GAP_LIMIT, None, ALU.is_gt).then_inc(flag_done, 1)

            def exact_shift(b):
                flat = pair[1][:, :, :].rearrange("p a q -> p (a q)")
                for m in range(NMAX):
                    h, qt = m // NT, m % NT
                    col = (h % 2) * 8 + h // 2
                    dve.wait_ge(max_ps, b * (NMAX + 1) + m + 1)
                    dve.tensor_tensor(flat[:, qt * P:(qt + 1) * P], flat[:, qt * P:(qt + 1) * P], causal, ALU.add
                                      ).then_inc(max_step, 1)
                    dve.wait_ge(max_step, b * NMAX + m + 1)
                    dve.tensor_reduce(row_max[:, qt, col:col + 1], flat[:, 0:(qt + 1) * P], AX.X, ALU.max
                                      ).then_inc(max_done, 1)
                dve.wait_ge(max_ps, b * (NMAX + 1) + NMAX + 1)
                heads = pair[0][0:H, :, :].rearrange("p a q -> p (a q)")
                dve.tensor_tensor(shift[:, :], shift[:, :].bitcast(F32), heads, ALU.subtract).then_inc(shift_done, 1)

            def settle_shift(b):
                dve.wait_ge(flag_done, b + 1)
                dve.memset(row_max[:, :, :], 0.0)
                loose = dve.value_load(flag[0:1, 0:1], min_val=0, max_val=1)
                with dve.If(loose > 0):
                    exact_shift(b)
                with dve.Else():
                    dve.sem_inc(max_done, NMAX)
                    dve.sem_inc(max_step, NMAX)
                    dve.sem_inc(shift_done, 1)

            def activate_h(b, i):
                dve.wait_ge(relu_done, b * NFC + i + 1)
                dve.tensor_tensor(h_sq[:, :], h_sq[:, :], h_sq[:, :], ALU.mult).then_inc(sq_h, 1)
                if i >= 2:
                    dve.wait_ge(proj_done, b * NFC + i - 1)
                dve.wait_ge(sq_h, b * NFC + i + 1)
                dve.tensor_copy(h_hi[i % 2][:, :], h_sq[:, :]).then_inc(h_hi_done, 1)

            def spikes(b, g, a, stages):
                base = ((b * NG + g) * 2 + a) * STEPS
                y = y_sb[:, a, :]
                for s in stages:
                    if s == 0:
                        dve.wait_ge(y_copied, b * 4 + g * 2 + a + 1)
                        if g or a:
                            dve.wait_ge(resid_done, b * 4 + g * 2 + a)
                        dve.tensor_scalar(count[:, :], y, edges[s], None, ALU.is_gt).then_inc(spike_step, 1)
                    elif s < STEPS:
                        dve.wait_ge(spike_step, base + s)
                        dve.scalar_tensor_tensor(count[:, :], y, edges[s], count[:, :], ALU.is_gt, ALU.add
                                                 ).then_inc(spike_step, 1)
                    else:
                        dve.wait_ge(xb_done, b * NT + NT)
                        dve.wait_ge(spike_step, base + STEPS)
                        tiles = slice(4 * g + 2 * a, 4 * g + 2 * a + 2)
                        dve.scalar_tensor_tensor(
                            resid[:, tiles, :], count[:, :].rearrange("p (t d) -> p t d", d=D), 1.0 / STEPS,
                            resid[:, tiles, :], ALU.mult, ALU.add).then_inc(resid_done, 1)

            def take_y(b, g):
                dve.wait_ge(proj_done, b * NFC + (g + 1) * NFT)
                if g:
                    dve.wait_ge(attn_done, b * KD + 1)
                for a in range(2):
                    dve.tensor_copy(y_sb[:, a, :], proj_bank[:, a, :]).then_inc(y_copied, 1)

            def take_numer(b, quad, g):
                dve.wait_ge(pv_done, b * NUNIT + quad * NU + GROUP_END[g] + 1)
                if g == 0 and quad >= 1:
                    dve.wait_ge(numer_in[(quad - 1) // 2], (b * 2 + (quad - 1) % 2 + 1) * 4 * 16)
                    dve.wait_ge(denom_in, (b * NQUAD + quad) * 16)
                dve.tensor_copy(numer[:, g * G:(g + 1) * G], pv_bank).then_inc(numer_done, 1)

            def projection(b, last):
                rotate(b, 0)
                low_xT(b, 2)
                low_xT(b, 3)
                if last is not None:
                    invert(last, 1)
                rotate(b, 1)
                low_qk(b, 0)
                rotate(b, 2)
                low_qk(b, 1)
                if last is not None:
                    divide(last, 1)
                rotate(b, 3)
                low_qk(b, 2)
                activate_h(b, 0)
                low_qk(b, 3)
                if last is not None:
                    finish(last, range(2))
                bound(b)
                if last is not None:
                    finish(last, range(2, 4))
                activate_h(b, 1)
                raise_flag(b)
                settle_shift(b)
                for i in range(2, FRONT):
                    activate_h(b, i)

            def attention(b, more):
                for n in STEPS_ALL:
                    for c, i, half in HALVES[n]:
                        if not c and half:
                            activate_h(b, i)
                    if n in GROUP_ENDS:
                        take_numer(b, *GROUP_ENDS[n])
                    if n in Y_AT:
                        take_y(b, Y_AT[n])
                    if n in SPIKES_AT:
                        spikes(b, *SPIKES_AT[n])
                    if n == INVERT_AT:
                        invert(b, 0)
                    if n == DIVIDE_AT:
                        divide(b, 0)
                    if more:
                        if STATS_AT <= n < STATS_AT + NT:
                            statistics(b + 1, n - STATS_AT)
                        if n == STATS_AT + NT:
                            variance(b + 1)
                        if XN_AT <= n < XN_AT + NT:
                            normalise(b + 1, n - XN_AT)
                        if n in XT_AT:
                            low_xT(b + 1, XT_AT[n])

            for t in range(NT):
                statistics(0, t)
            variance(0)
            for t in range(NT):
                normalise(0, t)
            for n in range(2):
                low_xT(0, n)
            projection(0, None)
            with dve.Fori(0, B - 1) as b:
                attention(b, True)
                projection(b + 1, b)
            attention(B - 1, False)
            invert(B - 1, 1)
            divide(B - 1, 1)
            finish(B - 1, range(4))

        @block.tensor
        def _(pe):
            def split_product(bank, parts):
                for n, (lhsT, rhs) in enumerate(parts):
                    ins = pe.matmul(bank, lhsT, rhs, start=n == 0, stop=n == len(parts) - 1)
                return ins

            def transpose(b, n, last):
                g, k = n // 2, n % 2
                pe.wait_ge(xn_done, b * NT + 4 * g + 4)
                if n == 3:
                    pe.wait_ge(xT_lo_done, b * 4 + 1)
                if n == 0 and last is not None:
                    pe.wait_ge(relu_done, last * NFC + NFC)
                if n == 1 and last is not None:
                    pe.wait_ge(exp_done, (last + 1) * NUNIT * 2 - 1)
                for t in range(4):
                    ins = pe.transpose(xT_bank[n][:, t * P:(t + 1) * P], xn[:, 4 * g + t, k * P:(k + 1) * P], ident)
                ins.then_inc(xT_ps, 1)

            def queries_keys(b, last):
                for u in range(4):
                    g, is_k = u // 2, u % 2
                    cols = slice(g * G, (g + 1) * G)
                    pe.wait_ge(xT_lo_done, b * 4 + (2 if u < 2 else 4))
                    if u == 0 and last is not None:
                        pe.wait_ge(exp_done, (last + 1) * NUNIT * 2)
                    if u == 1:
                        transpose(b, 2, last)
                        transpose(b, 3, last)
                        if last is not None:
                            pe.wait_ge(y_copied, last * 4 + 4)
                    if u == 3:
                        pe.wait_ge(rot_done, b * 4 + 1)
                    for eo in range(2):
                        m = slice((2 * is_k + eo) * P, (2 * is_k + eo + 1) * P)
                        parts = [p for k in range(KD) for p in (
                            (wqk_hi[:, k, m], xT_hi[:, k, cols]), (wqk_lo[:, k, m], xT_hi[:, k, cols]),
                            (wqk_hi[:, k, m], xT_lo[:, k, cols]))]
                        ins = split_product(pair[QK_PAIR[u]][:, eo, :], parts)
                    ins.then_inc(qk_ps, 1)

            def values(b, last):
                for t in range(NT):
                    n = t // 2
                    cols = slice(t * P, (t + 1) * P)
                    if t == 0:
                        pe.wait_ge(rot_done, b * 4 + 2)
                    if t == 4 and last is not None:
                        pe.wait_ge(numer_done, (last + 1) * NQUAD * 2)
                    parts = [p for k in range(KD) for p in (
                        (xT_hi[:, k, cols], wv_hi[:, k, :]), (xT_hi[:, k, cols], wv_lo[:, k, :]),
                        (xT_lo[:, k, cols], wv_hi[:, k, :]))]
                    ins = split_product(v_bank[n][:, (t % 2) * D:(t % 2 + 1) * D], parts)
                    if t % 2:
                        ins.then_inc(v_ps, 1)

            def output(b, next_b, tiles):
                pe.wait_ge(attn_done, b * KD + KD)
                for t in tiles:
                    n = t // 2
                    if next_b is not None and t == 0:
                        pe.wait_ge(rot_done, next_b * 4 + 3)
                    if next_b is not None and t == 4:
                        pe.wait_ge(rot_done, next_b * 4 + 4)
                    ins = split_product(pair[n // 2][:, n % 2, (t % 2) * D:(t % 2 + 1) * D],
                                        [(attn[:, k, t * P:(t + 1) * P], wo_sb[:, k, :]) for k in range(KD)])
                    if t % 2:
                        ins.then_inc(wo_ps, 1)

            def norms(b):
                pe.wait_ge(v_copied, b * 4 + 2)
                pe.wait_ge(sq_done, b * 4 + 4)
                pe.wait_ge(own_done, b * NG + NG)
                for g in range(NG):
                    q2, k2, own = (lambda eo: squares[:, 2 * g, eo, :], lambda eo: squares[:, 2 * g + 1, eo, :],
                                   lambda eo: own_qk[:, g, eo, :])
                    both = range(2)
                    split_product(pair[3][0:H, g, :], [(sel[:, 0, :], q2(eo)) for eo in both])
                    split_product(pair[3][64:64 + H, g, :], [(sel[:, 0, :], k2(eo)) for eo in both])
                    ins = split_product(pair[3][32:32 + H, g, :], [(sel[:, 1, :], q2(eo)) for eo in both]
                                        + [(sel[:, 2, :], own(eo)) for eo in both])
                ins.then_inc(norm_ps, 1)

            def row_maxima(b, last):
                flat = pair[1][:, :, :].rearrange("p a q -> p (a q)")
                for m in range(NMAX):
                    h, qt = m // NT, m % NT
                    rows = slice(64 * (h % 2), 64 * (h % 2) + 64)
                    if m == 0:
                        pe.wait_ge(shift_in, b * 2 * 16 + 16)
                        if last is not None:
                            pe.wait_ge(out_done, last * 4 + 4)
                        for s in stacked:
                            pe.wait_ge(s, (b + 1) * 2 * STACK_DMAS * 16)
                    else:
                        pe.wait_ge(max_done, b * NMAX + m)
                    for g in range(qt * P // G + 1):
                        w = min(G, (qt + 1) * P - g * G)
                        ins = pe.matmul(flat[:, g * G:g * G + w], q_stack[rows, h // 2, qt * P:(qt + 1) * P],
                                        k_stack[rows, h // 2, g * G:g * G + w], start=True, stop=True)
                    ins.then_inc(max_ps, 1)
                pe.wait_ge(max_done, (b + 1) * NMAX)
                for qt in range(NT):
                    ins = pe.transpose(pair[0][0:H, qt // 4, (qt % 4) * P:(qt % 4 + 1) * P], row_max[:, qt, :], ident)
                ins.then_inc(max_ps, 1)

            def expand(b, i, half):
                g, f = i // NFT, i % NFT
                cols, m = slice(g * G, (g + 1) * G), slice(f * P, (f + 1) * P)
                if half == 0:
                    if i == 0:
                        pe.wait_ge(v_copied, b * 4 + 4)
                    else:
                        pe.wait_ge(relu_done, b * NFC + i)
                k = half
                for n, (w, xT) in enumerate(((wfc_hi, xT_hi), (wfc_lo, xT_hi), (wfc_hi, xT_lo))):
                    ins = pe.matmul(fc_bank, w[:, k, m], xT[:, k, cols], start=half == 0 and n == 0,
                                    stop=half == 1 and n == 2)
                if half:
                    ins.then_inc(fc_ps, 1)

            def contract(b, i, half):
                g, f = i // NFT, i % NFT
                if half == 0:
                    if i == 0:
                        pe.wait_ge(norm_used, b * 3 + 3)
                    pe.wait_ge(h_lo_done, b * NFC + i + 1)
                if f == 0 and g:
                    pe.wait_ge(y_copied, b * 4 + half + 1)
                for a in range(2):
                    t = 2 * half + a
                    cols = slice(t * P, (t + 1) * P)
                    for n, (h, w) in enumerate(((h_hi, wproj_hi), (h_hi, wproj_lo), (h_lo, wproj_hi))):
                        ins = pe.matmul(proj_bank[:, half, a * D:(a + 1) * D], h[i % 2][:, cols], w[:, f, :],
                                        start=f == 0 and n == 0 and a == 0, stop=f == NFT - 1 and n == 2,
                                        skip_group_check=True)
                if half:
                    ins.then_inc(proj_done, 1)

            def whole(step, b, i):
                for half in range(2):
                    step(b, i, half)

            def projection(b, last):
                queries_keys(b, last)
                values(b, last)
                whole(expand, b, 0)
                if last is not None:
                    output(last, b, range(4))
                norms(b)
                if last is not None:
                    output(last, b, range(4, NT))
                whole(expand, b, 1)
                whole(contract, b, 0)
                alone(pe, flag_done, b + 1)
                loose = pe.value_load(flag[0:1, 0:1], min_val=0, max_val=1)
                with pe.If(loose > 0):
                    row_maxima(b, last)
                with pe.Else():
                    pe.sem_inc(max_ps, NMAX + 1)
                for i in range(2, FRONT):
                    whole(expand, b, i)
                    whole(contract, b, i - 1)

            def scores(b, n, last):
                quad, (kt, g) = n // NU, UNITS[n % NU]
                q0 = first_query(kt, g)
                for pr in range(2):
                    m = 2 * n + pr
                    if m >= NSLOT:
                        pe.wait_ge(exp_done, b * 2 * NUNIT + m - NSLOT + 1)
                    elif last is not None:
                        pe.wait_ge(out_done, last * 4 + 2 * m + 2)
                    for half in range(2):
                        rows = slice(64 * half, 64 * half + 64)
                        tile = 2 * quad + pr
                        ins = pe.matmul(pair[m % NSLOT][:, half, 0:width(n)],
                                        k_stack[rows, tile, kt * P:(kt + 1) * P], q_stack[rows, tile, q0:(g + 1) * G],
                                        start=True, stop=True)
                    ins.then_inc(scores_ps, 1)

            def weigh(b, n):
                quad, (kt, g) = n // NU, UNITS[n % NU]
                q0 = first_query(kt, g)
                first, end = kt == 0, n % NU in GROUP_END
                pe.wait_ge(exp_done, b * 2 * NUNIT + 2 * n + 2)
                if DIAG[n % NU]:
                    pe.wait_ge(mask_done, b * NQUAD * ND + diag_before(n) + 1)
                if n == 0:
                    pe.wait_ge(v_done, b * NT + NT)
                elif first:
                    pe.wait_ge(numer_done, b * NQUAD * 2 + quad * 2 + g)
                for i in range(4):
                    ins = pe.matmul(pv_bank[32 * i:32 * i + VW, q0 - g * G:G], v_sb[:, kt, 4 * quad + i, :],
                                    probs[n % NPB][:, i, 0:width(n)], start=first, stop=end, skip_group_check=True)
                ins.then_inc(pv_done, 1)

            def attention(b, last, more):
                for s in stacked:
                    pe.wait_ge(s, (b + 1) * 2 * STACK_DMAS * 16)
                pe.wait_ge(shift_in, (b + 1) * 2 * 16)
                for n in STEPS_ALL:
                    if n < NUNIT:
                        scores(b, n, last)
                    for c, i, half in HALVES[n]:
                        (contract if c else expand)(b, i, half)
                    if more and n in XT_AT:
                        transpose(b + 1, XT_AT[n], b)
                    if n >= LAG:
                        weigh(b, n - LAG)

            pe.wait_ge(w_split, 9)
            pe.wait_ge(consts_in, 16 * 6)
            pe.wait_ge(cleared, 3)
            for n in range(2):
                transpose(0, n, None)
            projection(0, None)
            with pe.Fori(0, B - 1) as b:
                attention(b, None, True)
                projection(b + 1, b)
            attention(B - 1, None, False)
            output(B - 1, None, range(NT))


def rotary_tables():
    inv_freq = (np.float32(1.0) / np.float32(THETA) ** (np.arange(0, DK, 2, dtype=np.float32) / np.float32(DK))).astype(np.float32)
    angles = np.arange(S, dtype=np.float32)[None, :] * inv_freq[:, None]
    rows = np.tile(np.repeat(np.arange(NF), NTILE), 2)
    return np.stack([np.cos(angles), np.sin(angles)]).astype(np.float32)[:, rows, :]


def fixed_masks():
    i = np.arange(P)
    ident = (i[:, None] == i[None, :]).astype(np.float32)
    causal = np.where(i[None, :] <= i[:, None], 0.0, MASKED).astype(np.float32)
    head = i // 64 * NTILE + i % NTILE
    mine = (head[:, None] == np.arange(H)[None, :]).astype(np.float32)
    return np.concatenate([ident, causal, mine, np.float32(BOUND_HALF) * mine, -mine], axis=1)


def kernel(**inputs):
    import concourse.bacc as _bacc
    from concourse.bass_utils import run_bass_kernel_spmd as _run

    a = {n.split("_", 1)[1]: np.ascontiguousarray(inputs[n]) for n in inputs}
    half, freq, tile = (v.ravel() for v in np.meshgrid(np.arange(2), np.arange(NF), np.arange(NTILE), indexing="ij"))
    column = (2 * tile + half) * DK + 2 * freq
    order = [column, column + 1]
    laid = {
        "x": a["attn_x"],
        "wqk": np.concatenate([a[w][o].T for w in ("attn_Wq", "attn_Wk") for o in order], axis=1),
        "bqk": np.stack([a[v][o] for v in ("attn_bq", "attn_bk") for o in order], axis=1),
        "wv": a["attn_Wv"].T,
        "bv": a["attn_bv"],
        "wfc": a["ffn_W_fc"].T,
        "wproj": a["ffn_W_proj"].T,
        "wo": a["attn_Wo"].T,
        "bo": a["attn_bo"],
        "tables": rotary_tables(),
        "consts": fixed_masks(),
    }
    nc = _bacc.Bacc("TRN2", target_bir_lowering=False, num_devices=1, dynamic_dma_scratch_size=1024)
    arrays, args = {}, []
    for name, v in laid.items():
        v = np.ascontiguousarray(v)
        arrays[f"in_{name}"] = v
        args.append(nc.dram_tensor(f"in_{name}", v.shape, mybir.dt.from_np(v.dtype), kind="ExternalInput").ap())
    args.append(nc.dram_tensor("out", (B, S, D), F32, kind="ExternalOutput").ap())
    layer_kernel(nc, *args)
    r = _run(nc, [arrays], core_ids=[0])
    return r.results[0]["out"]
```

```python
from contextlib import ExitStack

import numpy as np
import concourse.bass as bass
from concourse import mybir

F32, F32R, BF16, I32 = mybir.dt.float32, mybir.dt.float32r, mybir.dt.bfloat16, mybir.dt.int32
ALU, ACT, AX = mybir.AluOpType, mybir.ActivationFunctionType, mybir.AxisListType

P = 128
B, S, D = 16, 1024, 256
H, DK, F = 16, 16, 1024
NF = DK // 2
THETA, LN_EPS, SCALE = 10000.0, 1e-5, 1.0 / DK ** 0.5
BETA, THRESHOLD, STEPS = 0.9, 1.0, 5
NT = S // P
G = 512
NG = S // G
KD = D // P
NFT = F // P
NTILE = H // 2
NQUAD = H // 4
VW = DK + 1
BOUND_HALF = 131 / 256
GAP_LIMIT = 64.0 / SCALE
MASKED = -1e30

UNITS = [(0, 0), (3, 0), (2, 0), (1, 0), (0, 1), (7, 1), (6, 1), (5, 1), (4, 1), (1, 1), (2, 1), (3, 1)]
assert sorted(UNITS) == [(kt, g) for kt in range(NT) for g in range(NG) if (g + 1) * G > kt * P]
NU = len(UNITS)
NUNIT = NQUAD * NU
GROUP_END = [n for n in range(NU) if n + 1 == NU or UNITS[n + 1][1] != UNITS[n][1]]
DIAG = [kt // (G // P) == g for kt, g in UNITS]
ND = sum(DIAG)
LAG = 2
NPB = 3
NSLOT = 2


def first_query(kt, g):
    return max(kt * P, g * G)


def width(n):
    kt, g = UNITS[n % NU]
    return (g + 1) * G - first_query(kt, g)


def diag_before(n):
    return n // NU * ND + sum(DIAG[:n % NU])


NFC = NG * NFT
FRONT = 4
MLP_END = NUNIT - 4


def mlp_halves():
    items = [item for i in range(FRONT, NFC) for item in ((0, i), (1, i - 1))] + [(1, NFC - 1)]
    halves = [(c, i, half) for c, i in items for half in range(2)]
    share = [width(n) + G if n < MLP_END else 0 for n in range(NUNIT + LAG)]
    total, done, steps, taken = sum(share), 0, [], 0
    for n in range(NUNIT + LAG):
        done += share[n]
        upto = len(halves) * done // total
        steps.append(halves[taken:upto])
        taken = upto
    return steps


def spike_thresholds():
    f = np.float32

    def count(y):
        mem, spikes = f(0), 0
        for _ in range(STEPS):
            reset = f(mem - f(THRESHOLD) > 0)
            mem = f(f(f(BETA) * mem + y) - reset * f(THRESHOLD))
            spikes += bool(mem - f(THRESHOLD) > 0)
        return spikes

    edges = []
    for n in range(1, STEPS + 1):
        lo, hi = f(0), f(2)
        while np.nextafter(lo, hi) < hi:
            mid = f((lo + hi) / f(2))
            mid = mid if lo < mid < hi else np.nextafter(lo, hi)
            lo, hi = (lo, mid) if count(mid) >= n else (mid, hi)
        edges.append(float(lo))
    return edges


def layer_kernel(nc, x, wqk, bqk, wv, bv, wfc, wproj, wo, bo, tables, consts, selectors, out):
    edges = spike_thresholds()
    with ExitStack() as ctx:
        KB = 1024

        def here():
            return (nc.sbuf_base + 31) // 32 * 32

        arena_at = here()
        ctx.enter_context(nc.sbuf_tensor("arena", [P, 32 * KB // 4], F32))

        def shared(name, shape, dt, at):
            return nc.alloc_sbuf_tensor_at(name, shape, dt, offset=arena_at + at)

        def sb(name, shape, dt=F32):
            return ctx.enter_context(nc.sbuf_tensor(name, shape, dt))

        probs = [shared(f"probs{i}", [P, 4, G], F32, 8 * KB * i) for i in range(NPB)]
        planes = [shared(f"planes{i}", [P, 2, 2, G], F32R, 8 * KB * i) for i in range(2)]
        rot = [shared(f"rot{i}", [P, 2, G], F32, (16 + 4 * i) * KB) for i in range(2)]
        rot_b = [shared(f"rot_b{i}", [P, 2, G], F32, (24 + 4 * i) * KB) for i in range(2)]

        xn_at = here()
        xn = sb("xn", [P, NT, D])
        squares = nc.alloc_sbuf_tensor_at("squares", [P, 4, 2, G], BF16, offset=xn_at)
        row_max = nc.alloc_sbuf_tensor_at("row_max", [P, NT, NG * H], F32, offset=xn_at)

        h_sq_at = here()
        h_sq = [sb("h_sq0", [P, G]), shared("h_sq1", [P, G], F32, 24 * KB)]
        h_hi, h_lo = ([sb(f"{n}{i}", [P, G], F32R) for i in range(2)] for n in ("h_hi", "h_lo"))
        count = sb("count", [P, G], BF16)
        q_stack = sb("q_stack", [P, NTILE, S], F32R)
        k_stack = sb("k_stack", [P, NTILE, S], F32R)
        wqk_hi, wqk_lo = sb("wqk_hi", [P, KD, 4 * P], F32R), sb("wqk_lo", [P, KD, 4 * P], F32R)
        wv_hi, wv_lo = sb("wv_hi", [P, KD, D], F32R), sb("wv_lo", [P, KD, D], F32R)
        wfc_hi, wfc_lo = sb("wfc_hi", [P, KD, F], F32R), sb("wfc_lo", [P, KD, F], F32R)
        wproj_hi, wproj_lo = sb("wproj_hi", [P, NFT, D], F32R), sb("wproj_lo", [P, NFT, D], F32R)
        wo_sb = sb("wo_sb", [P, KD, D])
        table = sb("table", [P, 2, S])
        xT_hi, xT_lo = sb("xT_hi", [P, KD, S], F32R), sb("xT_lo", [P, KD, S], F32R)
        v_sb = sb("v_sb", [P, NT, H, VW])
        resid_at = here()
        resid = sb("resid", [P, NT, D])
        attn_at = here()
        attn = sb("attn", [P, KD, S])
        numer_at = here()
        numer = sb("numer", [P, S])
        shift = nc.alloc_sbuf_tensor_at("shift", [NG * H, G], F32R, offset=numer_at)
        sel_in = nc.alloc_sbuf_tensor_at("sel_in", [P, 9 * H], F32, offset=numer_at)
        own_qk = nc.alloc_sbuf_tensor_at("own_qk", [P, NG, 2, G], BF16, offset=numer_at)
        denom = sb("denom", [64, P])
        recip_at = here()
        recip_rows = sb("recip_rows", [P, S])
        y_sb = nc.alloc_sbuf_tensor_at("y_sb", [P, 2, G], F32, offset=recip_at)
        out_sb = [nc.alloc_sbuf_tensor_at(f"out_sb{i}", [P, 2, D], F32, offset=recip_at + 2 * KB * i) for i in range(2)]
        wqk_in, wv_in, wfc_in, wproj_in = (
            nc.alloc_sbuf_tensor_at(n, shape, F32, offset=at) for n, shape, at in (
                ("wqk_in", [P, KD, 4 * P], recip_at), ("wv_in", [P, KD, D], h_sq_at),
                ("wfc_in", [P, KD, F], resid_at), ("wproj_in", [P, NFT, D], attn_at)))
        const = sb("const", [P, 2 * P])
        ident, causal = const[:, 0:P], const[:, P:2 * P]
        sel = sb("sel", [P, 9 * H], BF16)
        by_one, by_half, by_minus = ([sel[:, (2 * i + 1 - g) * H:(2 * i + 3 - g) * H] for g in range(NG)] for i in range(3))
        by_one_twice = sel[:, 7 * H:9 * H]
        bqk_sb, neg_bqk = sb("bqk_sb", [P, 4]), sb("neg_bqk", [P, 4])
        bv_sb, bo_sb = sb("bv_sb", [P, D]), sb("bo_sb", [P, D])
        stats = sb("stats", [P, NT, 6])
        mean, var, mean_gap, rstd = (sb(n, [P, NT]) for n in ("mean", "var", "mean_gap", "rstd"))
        ln_a, ln_b, neg_half = (sb(n, [P, NT]) for n in ("ln_a", "ln_b", "neg_half"))
        bound_max = sb("bound_max", [P, 1])
        k_max, k_max1, q_gap, gap, gap_all = (sb(n, [NG * H, 1]) for n in ("k_max", "k_max1", "q_gap", "gap", "gap_all"))
        flag = sb("flag", [1, 1], I32)

        recip_dram = nc.dram_tensor("recip_dram", [KD, H // KD, S], F32, kind="Internal").ap()

        pair = [ctx.enter_context(nc.psum_tensor(f"pair{i}", [P, 2, G], F32)) for i in range(4)]
        pv_bank, fc_bank, proj_bank = pair[2][:, 0, :], pair[2][:, 1, :], pair[3]
        norm_bank = pv_bank
        xT_bank = (pair[2][:, 1, :], pair[0][:, 0, :], pair[0][:, 1, :], pair[2][:, 1, :])
        QK_PAIR = (1, 3, 0, 1)
        v_bank = (pair[3][:, 0, :], pair[2][:, 1, :], pair[2][:, 0, :], pair[3][:, 1, :])

        def sem(name):
            return ctx.enter_context(nc.semaphore(name))

        w_in = [sem(f"w_in_{n}") for n in ("qk", "v", "fc", "proj")]
        w_hi, w_lo = sem("w_hi"), sem("w_lo")
        consts_in, table_in, bias_in, wo_in = sem("consts_in"), sem("table_in"), sem("bias_in"), sem("wo_in")
        cleared, consts_done = sem("cleared"), sem("consts_done")
        x_in, resid_in = sem("x_in"), sem("resid_in")
        stats_done, var_done = sem("stats_done"), sem("var_done")
        ln_step, vec_step = sem("ln_step"), sem("vec_step")
        rstd_done, xn_done, xb_done = sem("rstd_done"), sem("xn_done"), sem("xb_done")
        xT_ps, xT_hi_done, xT_lo_done = sem("xT_ps"), sem("xT_hi_done"), sem("xT_lo_done")
        qk_ps, rot_done, rot_sum = sem("qk_ps"), sem("rot_done"), sem("rot_sum")
        plane_hi, plane_lo, sq_done = sem("plane_hi"), sem("plane_lo"), sem("sq_done")
        stacked = [sem("stacked0"), sem("stacked1")]
        v_ps, v_copied, v_done = sem("v_ps"), sem("v_copied"), sem("v_done")
        wo_ps, out_done = sem("wo_ps"), sem("out_done")
        out_sent = [sem("out_sent0"), sem("out_sent1")]
        own_done = [sem("own_done0"), sem("own_done1")]
        norm_ps, bound_step, norm_used, gap_done, gap_max, flag_done = (
            sem(n) for n in ("norm_ps", "bound_step", "norm_used", "gap_done", "gap_max", "flag_done"))
        max_ps, max_done, max_step = sem("max_ps"), sem("max_done"), sem("max_step")
        shift_done, shift_in, exact_in = sem("shift_done"), sem("shift_in"), sem("exact_in")
        fc_ps, relu_done, sq_h, h_hi_done, h_lo_done, proj_done = (
            sem(n) for n in ("fc_ps", "relu_done", "sq_h", "h_hi_done", "h_lo_done", "proj_done"))
        y_copied, spike_step, resid_done = sem("y_copied"), sem("spike_step"), sem("resid_done")
        scores_ps, exp_done, mask_done, pv_done = (
            sem(n) for n in ("scores_ps", "exp_done", "mask_done", "pv_done"))
        numer_done = sem("numer_done")
        numer_in = [sem("numer_in0"), sem("numer_in1")]
        denom_in, recip_done = sem("denom_in"), sem("recip_done")
        recip_out, recip_in, attn_done = sem("recip_out"), sem("recip_in"), sem("attn_done")
        NMAX = H * NT
        STACK_DMAS = 3 * 2

        HALVES = mlp_halves()
        STEPS_ALL = range(NUNIT + LAG)
        CONTRACTED = {i: n for n in STEPS_ALL for c, i, half in HALVES[n] if c and half}
        XT_AT = {NUNIT - 1: 0, NUNIT: 1}
        Y_AT = {CONTRACTED[g * NFT + NFT - 1]: g for g in range(NG)}
        SPIKES_AT = {CONTRACTED[g * NFT + NFT - 1] + 2 * a + part: (g, a, range(3 * part, 3 * part + 3))
                     for g in range(NG) for a in range(2) for part in range(2)}
        assert max(SPIKES_AT) < NUNIT + LAG
        GROUP_ENDS = {q * NU + n + LAG: (q, g) for q in range(NQUAD) for g, n in enumerate(GROUP_END)}
        STATS_AT, ROOT_AT, XN_AT, BO_AT = 4, 21, 24, 6
        INVERT_AT, DIVIDE_AT = 2 * NU + LAG + 3, 2 * NU + LAG + 9

        stood = sem("stood")

        def alone(eng, s, value):
            eng.wait_ge(s, value)
            eng.sem_inc(stood, 1)

        block = ctx.enter_context(nc.Block())

        @block.sync
        def _(sp):
            sp.dma_start(xn[:, :, :], x[0].rearrange("(t p) d -> p t d", p=P)).then_inc(x_in, 16)
            sp.dma_start(const[:, :], consts).then_inc(consts_in, 16)
            sp.dma_start(bqk_sb[:, :], bqk).then_inc(consts_in, 16)
            sp.dma_start(sel_in[:, :], selectors).then_inc(consts_in, 16)
            for n, (dst, src) in enumerate(((wqk_in, wqk), (wv_in, wv), (wfc_in, wfc), (wproj_in, wproj))):
                sp.dma_start(dst[:, :, :], src.rearrange("(k p) n -> p k n", p=P)).then_inc(w_in[n], 16)
                if n == 0:
                    sp.dma_start(table[:, :, :], tables.rearrange("t p s -> p t s")).then_inc(table_in, 16)
            sp.dma_start(bv_sb[:, :], bv.partition_broadcast(P)).then_inc(bias_in, 16)
            sp.dma_start(bo_sb[:, :], bo.partition_broadcast(P)).then_inc(bias_in, 16)
            sp.dma_start(wo_sb[:, :, :], wo.rearrange("(k p) n -> p k n", p=P)).then_inc(wo_in, 16)

            def load_x(b, last):
                alone(sp, norm_ps, last + 1)
                sp.dma_start(xn[:, :, :], x[b].rearrange("(t p) d -> p t d", p=P)).then_inc(x_in, 16)

            def load_resid(b):
                sp.dma_start(resid[:, :, :], x[b].rearrange("(t p) d -> p t d", p=P)).then_inc(resid_in, 16)

            def stack(b):
                for u in range(4):
                    g, is_k = u // 2, u % 2
                    dst = k_stack if is_k else q_stack
                    buf = planes[u % 2]
                    for lo in range(2):
                        sp.wait_ge(plane_lo if lo else plane_hi, b * 4 + u + 1)
                        for part in range(3):
                            if lo != (part == (1 if is_k else 2)):
                                continue
                            for eo in range(2):
                                sp.dma_start(dst[2 * part + eo:P:NF, :, g * G:(g + 1) * G].bitcast(F32),
                                             buf[:, lo, eo, :].bitcast(F32)).then_inc(stacked[u % 2], 16)

            def store(b, banks):
                for n in banks:
                    alone(sp, out_done, b * 4 + n + 1)
                    sp.dma_start(out[b].rearrange("(t p) d -> p t d", p=P)[:, 2 * n:2 * n + 2, :],
                                 out_sb[n % 2][:, :, :]).then_inc(out_sent[n % 2], 16)

            def stored(b):
                for s in out_sent:
                    alone(sp, s, (b + 1) * 2 * 16)

            def send_shift(landed):
                for g in range(NG):
                    sp.dma_start(q_stack[6:P:64, :, g * G:(g + 1) * G].bitcast(F32),
                                 shift[g * H:(g + 1) * H, :].bitcast(F32)).then_inc(landed, 16)

            def load_shift(b):
                sp.wait_ge(norm_used, b + 1)
                send_shift(shift_in)
                alone(sp, flag_done, b + 1)
                loose = sp.value_load(flag[0:1, 0:1], min_val=0, max_val=1)
                with sp.If(loose > 0):
                    alone(sp, shift_in, (b + 1) * NG * 16)
                    alone(sp, shift_done, b + 1)
                    send_shift(exact_in)
                with sp.Else():
                    sp.sem_inc(exact_in, NG * 16)

            def gather(b):
                for quad in range(NQUAD):
                    k, base = quad // 2, quad % 2 * 64
                    sp.wait_ge(numer_done, (b * NQUAD + quad) * 2 + 2)
                    sp.dma_start(denom[base // 2:base // 2 + 32, :], numer[DK:P:32, :]).then_inc(denom_in, 16)
                    for i in range(4):
                        sp.dma_start(attn[base + DK * i:base + DK * (i + 1), k, :],
                                     numer[32 * i:32 * i + DK, :]).then_inc(numer_in[k], 16)
                    if quad % 2:
                        sp.wait_ge(recip_done, b * KD + k + 1)
                        sp.dma_start(recip_dram[k].rearrange("h (c q) -> (h c) q", q=P), denom[:, :]
                                     ).then_inc(recip_out, 16)
                        alone(sp, recip_out, (b * KD + k + 1) * 16)
                        sp.dma_start(recip_rows[:, :],
                                     recip_dram[k].unsqueeze(1).broadcast_to([H // KD, DK, S])
                                     ).then_inc(recip_in, 16)

            sp.wait_ge(cleared, 3)
            stack(0)
            sp.wait_ge(w_lo, 3)
            load_resid(0)
            load_shift(0)
            with sp.Fori(0, B - 1) as b:
                load_x(b + 1, b)
                gather(b)
                stack(b + 1)
                store(b, range(2))
                load_shift(b + 1)
                store(b, range(2, 4))
                stored(b)
                load_resid(b + 1)
            gather(B - 1)
            store(B - 1, range(4))
            stored(B - 1)

        @block.gpsimd
        def _(pool):
            def chained(ins):
                ins.then_inc(ln_step, 1)

            pool.memset(v_sb[:, :, :, DK:VW], 1.0).then_inc(cleared, 1)
            pool.memset(neg_half[:, :], -0.5).then_inc(ln_step, 1)
            pool.memset(q_stack[:, :, :].bitcast(F32), 0.0).then_inc(cleared, 1)
            pool.wait_ge(ln_step, 1)
            LN_OPS = 5

            def root(b):
                base = b * LN_OPS + 1
                pool.wait_ge(var_done, b + 1)
                chained(pool.tensor_tensor(ln_a[:, :], var[:, :], neg_half[:, :], ALU.pow))
                pool.wait_ge(ln_step, base + 1)
                chained(pool.tensor_tensor(ln_b[:, :], ln_a[:, :], ln_a[:, :], ALU.mult))
                pool.wait_ge(ln_step, base + 2)
                chained(pool.tensor_tensor(ln_b[:, :], ln_b[:, :], var[:, :], ALU.mult))
                alone(pool, ln_step, base + 3)
                chained(pool.tensor_scalar(ln_b[:, :], ln_b[:, :], -0.5, 1.5, ALU.mult, ALU.add))
                pool.wait_ge(ln_step, base + 4)
                chained(pool.tensor_tensor(ln_b[:, :], ln_b[:, :], ln_a[:, :], ALU.mult))
                alone(pool, ln_step, base + 5)
                pool.tensor_copy(rstd[:, :], ln_b[:, :]).then_inc(rstd_done, 1)

            def add_bo(b, t):
                if t == 0:
                    pool.wait_ge(resid_in, b * 16 + 16)
                pool.tensor_tensor(resid[:, t, :], resid[:, t, :], bo_sb[:, :], ALU.add).then_inc(xb_done, 1)

            def add_bv(b, tiles):
                for t in tiles:
                    if t % 2 == 0:
                        pool.wait_ge(v_copied, b * 4 + t // 2 + 1)
                    heads = v_sb[:, t, :, 0:DK]
                    pool.tensor_tensor(heads, heads, bv_sb[:, :].rearrange("p (h d) -> p h d", d=DK), ALU.add
                                       ).then_inc(v_done, 1)

            def rotary(b, last):
                for u in range(4):
                    pool.wait_ge(rot_done, b * 4 + u + 1)
                    pool.tensor_tensor(rot[u % 2][:, :, :], rot[u % 2][:, :, :], rot_b[u % 2][:, :, :], ALU.add
                                       ).then_inc(rot_sum, 1)
                    if u == 1:
                        if last is not None:
                            pool.wait_ge(numer_in[1], (last + 1) * 2 * 4 * 16)
                            pool.wait_ge(denom_in, (last + 1) * NQUAD * 16)
                        pool.wait_ge(plane_hi, b * 4 + 2)
                        q, k = (planes[i][:, 0, :, :].bitcast(F32) for i in range(2))
                        pool.tensor_tensor(own_qk[:, 0, :, :], q, k, ALU.mult).then_inc(own_done[0], 1)

            def widest_gap(b):
                alone(pool, gap_done, b + 1)
                pool.partition_all_reduce(gap_all[:, :], gap[:, :], NG * H, bass.bass_isa.ReduceOp.max
                                          ).then_inc(gap_max, 1)

            def h_low(b, i):
                if i >= 2:
                    pool.wait_ge(proj_done, b * NFC + i - 1)
                pool.wait_ge(h_hi_done, b * NFC + i + 1)
                pool.tensor_tensor(h_lo[i % 2][:, :], h_sq[i % 2][:, :], h_hi[i % 2][:, :].bitcast(F32),
                                   ALU.subtract).then_inc(h_lo_done, 1)

            def mask(b, n):
                alone(pool, exp_done, (b * NUNIT + n) * 2 + 2)
                view = probs[n % NPB][:, :, 0:P]
                pool.affine_select(view, view, [[0, 4], [1, P]], ALU.is_ge, 0.0, base=0,
                                   channel_multiplier=-1).then_inc(mask_done, 1)

            def projection(b, last):
                rotary(b, last)
                add_bv(b, range(4))
                h_low(b, 0)
                h_low(b, 1)
                widest_gap(b)
                for i in range(2, FRONT):
                    h_low(b, i)

            def attention(b, more):
                for n in STEPS_ALL:
                    if n < NUNIT and DIAG[n % NU]:
                        mask(b, n)
                    for c, i, half in HALVES[n - 1] if n else ():
                        if not c and half:
                            h_low(b, i)
                    if n < NT // 2:
                        add_bv(b, [NT // 2 + n])
                    if BO_AT <= n < BO_AT + NT:
                        add_bo(b, n - BO_AT)
                    if n == ROOT_AT and more:
                        root(b + 1)

            root(0)
            pool.memset(k_stack[:, :, :].bitcast(F32), 1.0).then_inc(cleared, 1)
            pool.wait_ge(bias_in, 16 * 2)
            projection(0, None)
            with pool.Fori(0, B - 1) as b:
                attention(b, True)
                projection(b + 1, b)
            attention(B - 1, False)

        @block.scalar
        def _(act):
            def high_xT(b, n):
                g, k = n // 2, n % 2
                act.wait_ge(xT_ps, b * 4 + n + 1)
                act.activation(xT_hi[:, k, g * G:(g + 1) * G], xT_bank[n], ACT.Copy).then_inc(xT_hi_done, 1)

            def high_qk(b, u):
                act.wait_ge(rot_sum, b * 4 + u + 1)
                if u >= 2:
                    act.wait_ge(stacked[u % 2], (b * 2 + 1) * STACK_DMAS * 16)
                    act.wait_ge(own_done[0], b + 1)
                act.activation(planes[u % 2][:, 0, :, :], rot[u % 2][:, :, :], ACT.Copy).then_inc(plane_hi, 1)
                act.activation(squares[:, u, :, :], rot[u % 2][:, :, :], ACT.Square).then_inc(sq_done, 1)

            def take_v(b, n):
                act.wait_ge(v_ps, b * 4 + n + 1)
                act.activation(v_sb[:, 2 * n:2 * n + 2, :, 0:DK], v_bank[n].rearrange(
                    "p (t h d) -> p t h d", t=2, d=DK), ACT.Copy).then_inc(v_copied, 1)

            def rectify(b, i):
                if i >= 2:
                    act.wait_ge(h_lo_done, b * NFC + i - 1)
                act.wait_ge(fc_ps, b * NFC + i + 1)
                act.activation(h_sq[i % 2][:, :], fc_bank, ACT.Relu).then_inc(relu_done, 1)

            def projection(b):
                high_xT(b, 2)
                high_xT(b, 3)
                high_qk(b, 0)
                high_qk(b, 1)
                for n in range(4):
                    take_v(b, n)
                high_qk(b, 2)
                rectify(b, 0)
                high_qk(b, 3)
                for i in range(1, FRONT):
                    rectify(b, i)

            def attention(b, more):
                for n in STEPS_ALL:
                    if n < NUNIT:
                        w = width(n)
                        if n >= NPB:
                            act.wait_ge(pv_done, b * NUNIT + n - NPB + 1)
                        for pr in range(2):
                            m = 2 * n + pr
                            act.wait_ge(scores_ps, b * 2 * NUNIT + m + 1)
                            act.activation(probs[n % NPB][:, 2 * pr:2 * pr + 2, 0:w], pair[m % NSLOT][:, :, 0:w],
                                           ACT.Exp, scale=SCALE).then_inc(exp_done, 1)
                    for c, i, half in HALVES[n]:
                        if not c and half:
                            rectify(b, i)
                    if more and n in XT_AT:
                        high_xT(b + 1, XT_AT[n])

            for n, (hi, whole) in enumerate(((wqk_hi, wqk_in), (wv_hi, wv_in), (wfc_hi, wfc_in), (wproj_hi, wproj_in))):
                act.wait_ge(w_in[n], 16)
                act.activation(hi[:, :, :], whole[:, :, :], ACT.Copy).then_inc(w_hi, 1)
                if n == 1:
                    for k in range(2):
                        high_xT(0, k)
            projection(0)
            with act.Fori(0, B - 1) as b:
                attention(b, True)
                projection(b + 1)
            attention(B - 1, False)

        @block.vector
        def _(dve):
            weights = ((wqk_hi, wqk_lo, wqk_in), (wv_hi, wv_lo, wv_in), (wfc_hi, wfc_lo, wfc_in),
                       (wproj_hi, wproj_lo, wproj_in))

            def low_weight(n):
                hi, lo, whole = weights[n]
                dve.wait_ge(w_hi, n + 1)
                dve.tensor_tensor(lo[:, :, :], whole[:, :, :], hi[:, :, :].bitcast(F32), ALU.subtract).then_inc(w_lo, 1)

            def small_constants():
                dve.wait_ge(consts_in, 16 * 3)
                dve.tensor_copy(sel[:, :], sel_in[:, :]
                                ).then_inc(consts_done, 1)
                dve.tensor_scalar(neg_bqk[:, :], bqk_sb[:, :], -1.0, None, ALU.mult).then_inc(consts_done, 1)

            def statistics(b, t):
                if t == 0:
                    dve.wait_ge(x_in, b * 16 + 16)
                dve.bn_stats(stats[:, t, :], xn[:, t, :]).then_inc(stats_done, 1)

            def variance(b):
                base = b * 6
                dve.wait_ge(stats_done, b * NT + NT)
                dve.tensor_tensor(mean_gap[:, :], stats[:, :, 1], stats[:, :, 4], ALU.subtract).then_inc(vec_step, 1)
                dve.tensor_tensor(mean[:, :], stats[:, :, 1], stats[:, :, 4], ALU.add).then_inc(vec_step, 1)
                dve.tensor_tensor(var[:, :], stats[:, :, 2], stats[:, :, 5], ALU.add).then_inc(vec_step, 1)
                dve.wait_ge(vec_step, base + 3)
                dve.tensor_tensor(mean_gap[:, :], mean_gap[:, :], mean_gap[:, :], ALU.mult).then_inc(vec_step, 1)
                dve.tensor_scalar(mean[:, :], mean[:, :], 0.5, None, ALU.mult).then_inc(vec_step, 1)
                dve.tensor_scalar(var[:, :], var[:, :], 1.0 / D, LN_EPS, ALU.mult, ALU.add).then_inc(vec_step, 1)
                dve.wait_ge(vec_step, base + 6)
                dve.scalar_tensor_tensor(var[:, :], mean_gap[:, :], 0.25, var[:, :], ALU.mult, ALU.add
                                         ).then_inc(var_done, 1)

            def normalise(b, t):
                dve.wait_ge(rstd_done, b + 1)
                dve.tensor_scalar(xn[:, t, :], xn[:, t, :], mean[:, t:t + 1], rstd[:, t:t + 1],
                                  ALU.subtract, ALU.mult).then_inc(xn_done, 1)

            def low_xT(b, n):
                g, k = n // 2, n % 2
                cols = slice(g * G, (g + 1) * G)
                dve.wait_ge(xT_hi_done, b * 4 + n + 1)
                dve.tensor_tensor(xT_lo[:, k, cols], xT_bank[n], xT_hi[:, k, cols].bitcast(F32),
                                  ALU.subtract).then_inc(xT_lo_done, 1)

            def rotate(b, u):
                g, is_k = u // 2, u % 2
                cos, sin = (table[:, n, g * G:(g + 1) * G] for n in range(2))
                even, odd = (pair[QK_PAIR[u]][:, eo, :] for eo in range(2))
                e_bias, o_bias = (bqk_sb[:, 2 * is_k + eo:2 * is_k + eo + 1] for eo in range(2))
                neg_o_bias = neg_bqk[:, 2 * is_k + 1:2 * is_k + 2]
                dve.wait_ge(qk_ps, b * 4 + u + 1)
                if u >= 2:
                    dve.wait_ge(rot_sum, b * 4 + u - 1)
                    dve.wait_ge(sq_done, b * 4 + u - 1)
                    dve.wait_ge(plane_lo, b * 4 + u - 1)
                part = rot[u % 2]
                dve.scalar_tensor_tensor(part[:, 0, :], even, e_bias, cos, ALU.add, ALU.mult)
                dve.scalar_tensor_tensor(part[:, 1, :], even, e_bias, sin, ALU.add, ALU.mult)
                dve.scalar_tensor_tensor(rot_b[u % 2][:, 0, :], odd, neg_o_bias, sin, ALU.subtract, ALU.mult, reverse0=True)
                dve.scalar_tensor_tensor(rot_b[u % 2][:, 1, :], odd, o_bias, cos, ALU.add, ALU.mult).then_inc(rot_done, 1)

            def own_product(b):
                dve.wait_ge(plane_hi, b * 4 + 4)
                q, k = (planes[i][:, 0, :, :].bitcast(F32) for i in range(2))
                dve.tensor_tensor(own_qk[:, 1, :, :], q, k, ALU.mult).then_inc(own_done[1], 1)

            def low_qk(b, u):
                dve.wait_ge(plane_hi, b * 4 + u + 1)
                dve.tensor_tensor(planes[u % 2][:, 1, :, :], rot[u % 2][:, :, :],
                                  planes[u % 2][:, 0, :, :].bitcast(F32), ALU.subtract).then_inc(plane_lo, 1)

            def invert(b, k):
                dve.wait_ge(denom_in, (b * NQUAD + 2 * k + 2) * 16)
                dve.reciprocal(denom[:, :], denom[:, :]).then_inc(recip_done, 1)

            def divide(b, k):
                dve.wait_ge(numer_in[k], (b + 1) * 2 * 4 * 16)
                dve.wait_ge(recip_in, (b * KD + k + 1) * 16)
                dve.tensor_tensor(attn[:, k, :], attn[:, k, :], recip_rows[:, :], ALU.mult).then_inc(attn_done, 1)

            def finish(b, banks):
                for n in banks:
                    if n >= 2:
                        dve.wait_ge(out_sent[n % 2], (b * 2 + 1) * 16)
                    dve.wait_ge(wo_ps, b * 4 + n + 1)
                    dve.tensor_tensor(out_sb[n % 2][:, :, :], pair[n // 2][:, n % 2, :].rearrange(
                        "p (t d) -> p t d", d=D), resid[:, 2 * n:2 * n + 2, :], ALU.add).then_inc(out_done, 1)

            def bound(b):
                dve.wait_ge(norm_ps, b + 1)
                dve.tensor_reduce(bound_max[:, :], norm_bank, AX.X, ALU.max).then_inc(bound_step, 1)
                dve.wait_ge(bound_step, b * 5 + 1)
                for part, to in ((1, q_gap), (2, k_max), (3, k_max1)):
                    dve.tensor_copy(to[:, :], bound_max[32 * part:32 * part + 32, :]).then_inc(bound_step, 1)
                dve.wait_ge(bound_step, b * 5 + 4)
                dve.tensor_tensor(k_max[:, :], k_max[:, :], k_max1[:, :], ALU.max).then_inc(bound_step, 1)
                dve.wait_ge(bound_step, b * 5 + 5)
                dve.scalar_tensor_tensor(gap[:, :], k_max[:, :], BOUND_HALF, q_gap[:, :], ALU.mult, ALU.add
                                         ).then_inc(gap_done, 1)
                dve.tensor_scalar(shift[:, :], norm_bank[0:32, :], k_max[:, 0:1], -BOUND_HALF, ALU.add, ALU.mult
                                  ).then_inc(norm_used, 1)

            def raise_flag(b):
                dve.wait_ge(gap_max, b + 1)
                dve.tensor_scalar(flag[:, :], gap_all[0:1, :], GAP_LIMIT, None, ALU.is_gt).then_inc(flag_done, 1)

            def exact_shift(b):
                flat = pair[0][:, :, :].rearrange("p a q -> p (a q)")
                dve.memset(row_max[:, :, :], 0.0).then_inc(max_step, 1)
                for m in range(NMAX):
                    h, qt = m // NT, m % NT
                    col = qt // (NT // NG) * H + (h % 2) * NTILE + h // 2
                    dve.wait_ge(max_ps, b * (NMAX + 1) + m + 1)
                    dve.tensor_tensor(flat[:, qt * P:(qt + 1) * P], flat[:, qt * P:(qt + 1) * P], causal, ALU.add
                                      ).then_inc(max_step, 1)
                    dve.wait_ge(max_step, b * (NMAX + 1) + m + 2)
                    dve.tensor_reduce(row_max[:, qt, col:col + 1], flat[:, 0:(qt + 1) * P], AX.X, ALU.max
                                      ).then_inc(max_done, 1)
                dve.wait_ge(max_ps, b * (NMAX + 1) + NMAX + 1)
                dve.tensor_tensor(shift[:, :], shift[:, :].bitcast(F32), pair[0][0:NG * H, 0, :], ALU.subtract
                                  ).then_inc(shift_done, 1)

            def settle_shift(b):
                alone(dve, flag_done, b + 1)
                loose = dve.value_load(flag[0:1, 0:1], min_val=0, max_val=1)
                with dve.If(loose > 0):
                    exact_shift(b)
                with dve.Else():
                    dve.sem_inc(max_done, NMAX)
                    dve.sem_inc(max_step, NMAX + 1)
                    dve.sem_inc(shift_done, 1)

            def activate_h(b, i):
                dve.wait_ge(relu_done, b * NFC + i + 1)
                dve.tensor_tensor(h_sq[i % 2][:, :], h_sq[i % 2][:, :], h_sq[i % 2][:, :], ALU.mult).then_inc(sq_h, 1)
                if i >= 2:
                    dve.wait_ge(proj_done, b * NFC + i - 1)
                dve.wait_ge(sq_h, b * NFC + i + 1)
                dve.tensor_copy(h_hi[i % 2][:, :], h_sq[i % 2][:, :]).then_inc(h_hi_done, 1)

            def spikes(b, g, a, stages):
                base = ((b * NG + g) * 2 + a) * STEPS
                y = y_sb[:, a, :]
                for s in stages:
                    if s == 0:
                        dve.wait_ge(y_copied, b * 4 + g * 2 + a + 1)
                        if g or a:
                            dve.wait_ge(resid_done, b * 4 + g * 2 + a)
                        dve.tensor_scalar(count[:, :], y, edges[s], None, ALU.is_gt).then_inc(spike_step, 1)
                    elif s < STEPS:
                        dve.wait_ge(spike_step, base + s)
                        dve.scalar_tensor_tensor(count[:, :], y, edges[s], count[:, :], ALU.is_gt, ALU.add
                                                 ).then_inc(spike_step, 1)
                    else:
                        dve.wait_ge(xb_done, b * NT + NT)
                        dve.wait_ge(spike_step, base + STEPS)
                        tiles = slice(4 * g + 2 * a, 4 * g + 2 * a + 2)
                        dve.scalar_tensor_tensor(
                            resid[:, tiles, :], count[:, :].rearrange("p (t d) -> p t d", d=D), 1.0 / STEPS,
                            resid[:, tiles, :], ALU.mult, ALU.add).then_inc(resid_done, 1)

            def take_y(b, g):
                dve.wait_ge(proj_done, b * NFC + (g + 1) * NFT)
                if g == 0:
                    dve.wait_ge(xb_done, b * NT + NT)
                else:
                    dve.wait_ge(attn_done, b * KD + 1)
                for a in range(2):
                    dve.tensor_copy(y_sb[:, a, :], proj_bank[:, a, :]).then_inc(y_copied, 1)

            def take_numer(b, quad, g):
                dve.wait_ge(pv_done, b * NUNIT + quad * NU + GROUP_END[g] + 1)
                if g == 0 and quad >= 1:
                    dve.wait_ge(numer_in[(quad - 1) // 2], (b * 2 + (quad - 1) % 2 + 1) * 4 * 16)
                    dve.wait_ge(denom_in, (b * NQUAD + quad) * 16)
                dve.tensor_copy(numer[:, g * G:(g + 1) * G], pv_bank).then_inc(numer_done, 1)

            def projection(b, last):
                low_xT(b, 2)
                low_xT(b, 3)
                rotate(b, 0)
                if last is not None:
                    invert(last, 1)
                rotate(b, 1)
                low_qk(b, 0)
                rotate(b, 2)
                low_qk(b, 1)
                if last is not None:
                    divide(last, 1)
                else:
                    low_weight(2)
                rotate(b, 3)
                low_qk(b, 2)
                if last is None:
                    low_weight(3)
                activate_h(b, 0)
                own_product(b)
                low_qk(b, 3)
                if last is not None:
                    finish(last, range(2))
                activate_h(b, 1)
                bound(b)
                activate_h(b, 2)
                raise_flag(b)
                settle_shift(b)
                if last is not None:
                    finish(last, range(2, 4))
                for i in range(3, FRONT):
                    activate_h(b, i)

            def attention(b, more):
                for n in STEPS_ALL:
                    if n in GROUP_ENDS:
                        take_numer(b, *GROUP_ENDS[n])
                    if n in Y_AT:
                        take_y(b, Y_AT[n])
                    if n in SPIKES_AT:
                        spikes(b, *SPIKES_AT[n])
                    if n == INVERT_AT:
                        invert(b, 0)
                    if n == DIVIDE_AT:
                        divide(b, 0)
                    if more:
                        if STATS_AT <= n < STATS_AT + NT:
                            statistics(b + 1, n - STATS_AT)
                        if n == STATS_AT + NT:
                            variance(b + 1)
                        if XN_AT <= n < XN_AT + NT:
                            normalise(b + 1, n - XN_AT)
                        if n in XT_AT:
                            low_xT(b + 1, XT_AT[n])
                    for c, i, half in HALVES[n]:
                        if not c and half:
                            activate_h(b, i)

            for t in range(NT):
                statistics(0, t)
            variance(0)
            small_constants()
            low_weight(0)
            low_weight(1)
            for t in range(NT):
                normalise(0, t)
            for n in range(2):
                low_xT(0, n)
            dve.wait_ge(table_in, 16)
            dve.wait_ge(consts_done, 2)
            projection(0, None)
            with dve.Fori(0, B - 1) as b:
                attention(b, True)
                projection(b + 1, b)
            attention(B - 1, False)
            invert(B - 1, 1)
            divide(B - 1, 1)
            finish(B - 1, range(4))

        @block.tensor
        def _(pe):
            def split_product(bank, parts):
                for n, (lhsT, rhs) in enumerate(parts):
                    ins = pe.matmul(bank, lhsT, rhs, start=n == 0, stop=n == len(parts) - 1)
                return ins

            def transpose(b, n, last):
                g, k = n // 2, n % 2
                pe.wait_ge(xn_done, b * NT + 4 * g + 4)
                if n == 3:
                    pe.wait_ge(xT_lo_done, b * 4 + 1)
                if n == 0 and last is not None:
                    pe.wait_ge(relu_done, last * NFC + NFC)
                if n == 1 and last is not None:
                    pe.wait_ge(exp_done, (last + 1) * NUNIT * 2 - 1)
                for t in range(4):
                    ins = pe.transpose(xT_bank[n][:, t * P:(t + 1) * P], xn[:, 4 * g + t, k * P:(k + 1) * P], ident)
                ins.then_inc(xT_ps, 1)

            def queries_keys(b, last):
                for u in range(4):
                    g, is_k = u // 2, u % 2
                    cols = slice(g * G, (g + 1) * G)
                    pe.wait_ge(xT_lo_done, b * 4 + (2 if u < 2 else 4))
                    if u == 0 and last is not None:
                        pe.wait_ge(exp_done, (last + 1) * NUNIT * 2)
                    if u == 0:
                        transpose(b, 2, last)
                        transpose(b, 3, last)
                    if u == 1:
                        if last is not None:
                            pe.wait_ge(y_copied, last * 4 + 4)
                    if u == 3:
                        pe.wait_ge(rot_done, b * 4 + 1)
                    for eo in range(2):
                        m = slice((2 * is_k + eo) * P, (2 * is_k + eo + 1) * P)
                        parts = [p for k in range(KD) for p in (
                            (wqk_hi[:, k, m], xT_hi[:, k, cols]), (wqk_lo[:, k, m], xT_hi[:, k, cols]),
                            (wqk_hi[:, k, m], xT_lo[:, k, cols]))]
                        ins = split_product(pair[QK_PAIR[u]][:, eo, :], parts)
                    ins.then_inc(qk_ps, 1)

            def values(b, last):
                for t in range(NT):
                    n = t // 2
                    cols = slice(t * P, (t + 1) * P)
                    if t == 0:
                        pe.wait_ge(rot_done, b * 4 + 2)
                    if t == 4 and last is not None:
                        pe.wait_ge(numer_done, (last + 1) * NQUAD * 2)
                    parts = [p for k in range(KD) for p in (
                        (xT_hi[:, k, cols], wv_hi[:, k, :]), (xT_hi[:, k, cols], wv_lo[:, k, :]),
                        (xT_lo[:, k, cols], wv_hi[:, k, :]))]
                    ins = split_product(v_bank[n][:, (t % 2) * D:(t % 2 + 1) * D], parts)
                    if t % 2:
                        ins.then_inc(v_ps, 1)

            def output(b, next_b, tiles):
                pe.wait_ge(attn_done, b * KD + KD)
                for t in tiles:
                    n = t // 2
                    if next_b is not None and t == 0:
                        pe.wait_ge(rot_done, next_b * 4 + 3)
                    if next_b is not None and t == 4:
                        pe.wait_ge(rot_done, next_b * 4 + 4)
                    ins = split_product(pair[n // 2][:, n % 2, (t % 2) * D:(t % 2 + 1) * D],
                                        [(attn[:, k, t * P:(t + 1) * P], wo_sb[:, k, :]) for k in range(KD)])
                    if t % 2:
                        ins.then_inc(wo_ps, 1)

            def norms(b):
                pe.wait_ge(v_copied, b * 4 + 3)
                pe.wait_ge(sq_done, b * 4 + 4)
                for s in own_done:
                    pe.wait_ge(s, b + 1)
                both = [(g, eo) for g in range(NG) for eo in range(2)]
                split_product(norm_bank[0:32, :], [(by_one[g], squares[:, 2 * g, eo, :]) for g, eo in both])
                split_product(norm_bank[32:64, :], [(by_half[g], squares[:, 2 * g, eo, :]) for g, eo in both]
                              + [(by_minus[g], own_qk[:, g, eo, :]) for g, eo in both])
                split_product(norm_bank[64:96, :], [(by_one_twice, squares[:, 1, eo, :]) for eo in range(2)])
                ins = split_product(norm_bank[96:128, :], [(by_one[1], squares[:, 3, eo, :]) for eo in range(2)])
                ins.then_inc(norm_ps, 1)

            def row_maxima(b, last):
                flat = pair[0][:, :, :].rearrange("p a q -> p (a q)")
                for m in range(NMAX):
                    h, qt = m // NT, m % NT
                    rows = slice(64 * (h % 2), 64 * (h % 2) + 64)
                    if m == 0:
                        pe.wait_ge(shift_in, (b + 1) * NG * 16)
                        if last is not None:
                            pe.wait_ge(out_done, last * 4 + 2)
                        for s in stacked:
                            pe.wait_ge(s, (b + 1) * 2 * STACK_DMAS * 16)
                    else:
                        pe.wait_ge(max_done, b * NMAX + m)
                    for g in range(qt * P // G + 1):
                        w = min(G, (qt + 1) * P - g * G)
                        ins = pe.matmul(flat[:, g * G:g * G + w], q_stack[rows, h // 2, qt * P:(qt + 1) * P],
                                        k_stack[rows, h // 2, g * G:g * G + w], start=True, stop=True)
                    ins.then_inc(max_ps, 1)
                pe.wait_ge(max_done, (b + 1) * NMAX)
                for t in range(NT // NG):
                    for g in range(NG):
                        ins = pe.matmul(pair[0][0:NG * H, 0, t * P:(t + 1) * P], row_max[:, g * (NT // NG) + t, :], ident,
                                        start=g == 0, stop=g == NG - 1)
                ins.then_inc(max_ps, 1)

            def expand(b, i, half):
                g, f = i // NFT, i % NFT
                cols, m = slice(g * G, (g + 1) * G), slice(f * P, (f + 1) * P)
                if half == 0:
                    if i == 0:
                        pe.wait_ge(v_copied, b * 4 + 2)
                    else:
                        pe.wait_ge(relu_done, b * NFC + i)
                k = half
                for n, (w, xT) in enumerate(((wfc_hi, xT_hi), (wfc_lo, xT_hi), (wfc_hi, xT_lo))):
                    ins = pe.matmul(fc_bank, w[:, k, m], xT[:, k, cols], start=half == 0 and n == 0,
                                    stop=half == 1 and n == 2)
                if half:
                    ins.then_inc(fc_ps, 1)

            def contract(b, i, half):
                g, f = i // NFT, i % NFT
                if half == 0:
                    if i == 0:
                        pe.wait_ge(v_copied, b * 4 + 4)
                    pe.wait_ge(h_lo_done, b * NFC + i + 1)
                if f == 0 and g:
                    pe.wait_ge(y_copied, b * 4 + half + 1)
                for a in range(2):
                    t = 2 * half + a
                    cols = slice(t * P, (t + 1) * P)
                    for n, (h, w) in enumerate(((h_hi, wproj_hi), (h_hi, wproj_lo), (h_lo, wproj_hi))):
                        ins = pe.matmul(proj_bank[:, half, a * D:(a + 1) * D], h[i % 2][:, cols], w[:, f, :],
                                        start=f == 0 and n == 0 and a == 0, stop=f == NFT - 1 and n == 2,
                                        skip_group_check=True)
                if half:
                    ins.then_inc(proj_done, 1)

            def whole(step, b, i):
                for half in range(2):
                    step(b, i, half)

            def projection(b, last):
                if last is None:
                    pe.wait_ge(w_lo, 1)
                queries_keys(b, last)
                if last is None:
                    pe.wait_ge(w_lo, 2)
                values(b, last)
                if last is None:
                    pe.wait_ge(w_lo, 3)
                    pe.wait_ge(consts_done, 2)
                whole(expand, b, 0)
                if last is not None:
                    output(last, b, range(4))
                whole(expand, b, 1)
                if last is not None:
                    output(last, b, range(4, 6))
                norms(b)
                if last is None:
                    pe.wait_ge(w_lo, 4)
                whole(contract, b, 0)
                whole(expand, b, 2)
                if last is not None:
                    output(last, b, range(6, NT))
                whole(contract, b, 1)
                alone(pe, flag_done, b + 1)
                loose = pe.value_load(flag[0:1, 0:1], min_val=0, max_val=1)
                with pe.If(loose > 0):
                    row_maxima(b, last)
                    alone(pe, exact_in, (b + 1) * NG * 16)
                with pe.Else():
                    pe.sem_inc(max_ps, NMAX + 1)
                for i in range(3, FRONT):
                    whole(expand, b, i)
                    whole(contract, b, i - 1)
                if last is not None:
                    pe.wait_ge(out_done, last * 4 + 4)

            def scores(b, n, pr):
                kt, g = UNITS[n % NU]
                q0, m, tile = first_query(kt, g), 2 * n + pr, 2 * (n // NU) + pr
                if m >= NSLOT:
                    pe.wait_ge(exp_done, b * 2 * NUNIT + m - NSLOT + 1)
                for half in range(2):
                    rows = slice(64 * half, 64 * half + 64)
                    ins = pe.matmul(pair[m % NSLOT][:, half, 0:width(n)],
                                    k_stack[rows, tile, kt * P:(kt + 1) * P], q_stack[rows, tile, q0:(g + 1) * G],
                                    start=True, stop=True)
                ins.then_inc(scores_ps, 1)

            def weigh(b, n):
                quad, (kt, g) = n // NU, UNITS[n % NU]
                q0 = first_query(kt, g)
                first, end = kt == 0, n % NU in GROUP_END
                pe.wait_ge(exp_done, b * 2 * NUNIT + 2 * n + 2)
                if DIAG[n % NU]:
                    pe.wait_ge(mask_done, b * NQUAD * ND + diag_before(n) + 1)
                if n == 0:
                    pe.wait_ge(v_done, b * NT + NT // 2)
                    pe.wait_ge(norm_used, b + 1)
                elif first:
                    pe.wait_ge(numer_done, b * NQUAD * 2 + quad * 2 + g)
                    if n == GROUP_END[0] + 1:
                        pe.wait_ge(v_done, b * NT + NT)
                for i in range(4):
                    ins = pe.matmul(pv_bank[32 * i:32 * i + VW, q0 - g * G:G], v_sb[:, kt, 4 * quad + i, :],
                                    probs[n % NPB][:, i, 0:width(n)], start=first, stop=end, skip_group_check=True)
                ins.then_inc(pv_done, 1)

            def attention(b, more):
                for s in stacked:
                    pe.wait_ge(s, (b + 1) * 2 * STACK_DMAS * 16)
                pe.wait_ge(shift_in, (b + 1) * NG * 16)
                for n in STEPS_ALL:
                    halves = list(HALVES[n])
                    for pr in range(2):
                        if n < NUNIT:
                            scores(b, n, pr)
                        for c, i, half in halves[:1] if pr == 0 else halves[1:]:
                            (contract if c else expand)(b, i, half)
                    if more and n in XT_AT:
                        transpose(b + 1, XT_AT[n], b)
                    if n >= LAG:
                        weigh(b, n - LAG)

            pe.wait_ge(consts_in, 16 * 3)
            for n in range(2):
                transpose(0, n, None)
            projection(0, None)
            pe.wait_ge(wo_in, 16)
            with pe.Fori(0, B - 1) as b:
                attention(b, True)
                projection(b + 1, b)
            attention(B - 1, False)
            output(B - 1, None, range(NT))


def rotary_tables():
    inv_freq = (np.float32(1.0) / np.float32(THETA) ** (np.arange(0, DK, 2, dtype=np.float32) / np.float32(DK))).astype(np.float32)
    angles = np.arange(S, dtype=np.float32)[None, :] * inv_freq[:, None]
    rows = np.tile(np.repeat(np.arange(NF), NTILE), 2)
    return np.stack([np.cos(angles), np.sin(angles)]).astype(np.float32)[:, rows, :]


def fixed_masks():
    i = np.arange(P)
    ident = (i[:, None] == i[None, :]).astype(np.float32)
    causal = np.where(i[None, :] <= i[:, None], 0.0, MASKED).astype(np.float32)
    head = i // 64 * NTILE + i % NTILE
    mine = (head[:, None] == np.arange(H)[None, :]).astype(np.float32)
    zero = np.zeros_like(mine)
    sel = [zero, mine, zero, np.float32(BOUND_HALF) * mine, zero, -mine, zero, mine, mine]
    return np.concatenate([ident, causal], axis=1), np.concatenate(sel, axis=1)


def kernel(**inputs):
    import concourse.bacc as _bacc
    from concourse.bass_utils import run_bass_kernel_spmd as _run

    a = {n.split("_", 1)[1]: np.ascontiguousarray(inputs[n]) for n in inputs}
    half, freq, tile = (v.ravel() for v in np.meshgrid(np.arange(2), np.arange(NF), np.arange(NTILE), indexing="ij"))
    column = (2 * tile + half) * DK + 2 * freq
    order = [column, column + 1]
    laid = {
        "x": a["attn_x"],
        "wqk": np.concatenate([a[w][o].T for w in ("attn_Wq", "attn_Wk") for o in order], axis=1),
        "bqk": np.stack([a[v][o] for v in ("attn_bq", "attn_bk") for o in order], axis=1),
        "wv": a["attn_Wv"].T,
        "bv": a["attn_bv"],
        "wfc": a["ffn_W_fc"].T,
        "wproj": a["ffn_W_proj"].T,
        "wo": a["attn_Wo"].T,
        "bo": a["attn_bo"],
        "tables": rotary_tables(),
        "consts": fixed_masks()[0],
        "selectors": fixed_masks()[1],
    }
    nc = _bacc.Bacc("TRN2", target_bir_lowering=False, num_devices=1, dynamic_dma_scratch_size=1024)
    arrays, args = {}, []
    for name, v in laid.items():
        v = np.ascontiguousarray(v)
        arrays[f"in_{name}"] = v
        args.append(nc.dram_tensor(f"in_{name}", v.shape, mybir.dt.from_np(v.dtype), kind="ExternalInput").ap())
    args.append(nc.dram_tensor("out", (B, S, D), F32, kind="ExternalOutput").ap())
    layer_kernel(nc, *args)
    r = _run(nc, [arrays], core_ids=[0])
    return r.results[0]["out"]
```
